# Optimizing a Trainium2 kernel written in Bass

```python
import numpy as np
import jax
import jax.numpy as jnp

def _softmax(x, axis=-1):
    return jax.nn.softmax(x, axis=axis)

def _gelu(x):
    return jax.nn.gelu(x, approximate=True)

def _silu(x):
    return jax.nn.silu(x)

def _sigmoid(x):
    return jax.nn.sigmoid(x)

def _layernorm(x, axis=-1, eps=1e-05):
    m = jnp.mean(x, axis=axis, keepdims=True)
    v = jnp.var(x, axis=axis, keepdims=True)
    return (x - m) / jnp.sqrt(v + eps)

def _scatter_add(tgt, idx, src, axis=0):
    return tgt.at[idx].add(src)

def _segment_sum(src, seg, n):
    return jax.ops.segment_sum(src, seg, n)
kernel_name = 'mk_adj_resnorm_d4_adj_r2_f30623'

def setup_inputs(seed: int=0):
    np.random.seed(seed)
    _w = jnp.asarray

    def _rec_inputs():
        import jax
        import jax.numpy as jnp
        _gk = jax.random.key(seed)
        x = 0.0002279 + 0.9999 * jax.random.normal(jax.random.fold_in(_gk, 1), (4096, 128), jnp.float32)
        _a = jax.random.bernoulli(jax.random.fold_in(_gk, 2), 0.000976562, (4096, 4096))
        adj = _a.astype(jnp.int32)
        return (x, adj)
    x, adj = _rec_inputs()

    def _L0_gnn_setup():
        import jax, jax.numpy as jnp
        import numpy as np
        N, D = (4096, 128)
        key = jax.random.key(seed)
        k1, k2, k3 = jax.random.split(key, 3)
        adj = jax.random.randint(k1, (N, N), 0, 2, dtype=jnp.int32)
        emb = jax.random.normal(k2, (N, D), dtype=jnp.float32)
        attn = jax.random.normal(k3, (2 * D, 1), dtype=jnp.float32)
        return {'adj': adj, 'emb': emb, 'attn': attn}
    _L0_gnn_all = _L0_gnn_setup()
    _L0_gnn_in = {k: v for k, v in _L0_gnn_all.items() if k in ('attn',)}
    del _L0_gnn_all

    def _L1_gnn_setup():
        import jax
        import jax.numpy as jnp
        import numpy as np
        from jax import lax
        N = 4096
        F = 128
        CHUNK = 64
        key = jax.random.key(seed)
        kx, ka = jax.random.split(key)
        X = jax.random.normal(kx, (N, F), dtype=jnp.float32)
        adj = jax.random.randint(ka, (N, N), 0, 2, dtype=jnp.int32)
        return {'X': X, 'adj': adj}
    _L1_gnn_all = _L1_gnn_setup()
    _L1_gnn_in = {k: v for k, v in _L1_gnn_all.items() if k in ()}
    del _L1_gnn_all

    def _L2_gnn_setup():
        import jax, jax.numpy as jnp
        import numpy as np
        from jax import lax
        N = 4096
        D = 128
        CHUNK = 128
        key = jax.random.key(seed)
        k1, k2 = jax.random.split(key)
        x = jax.random.normal(k1, (N, D), dtype=jnp.float32)
        adj = jax.random.randint(k2, (N, N), 0, 2, dtype=jnp.int32)
        return {'x': x, 'adj': adj}
    _L2_gnn_all = _L2_gnn_setup()
    _L2_gnn_in = {k: v for k, v in _L2_gnn_all.items() if k in ()}
    del _L2_gnn_all

    def _L3_gnn_setup():
        import jax, jax.numpy as jnp
        import numpy as np
        NEG_INF = -9000000000000000.0
        ALPHA = 0.2
        key = jax.random.key(seed)
        k1, k2, k3, k4 = jax.random.split(key, 4)
        N, F_in, F_out = (4096, 128, 128)
        x = jax.random.normal(k1, (N, F_in), dtype=jnp.float32)
        adj = jax.random.randint(k2, (N, N), 0, 2, dtype=jnp.int32)
        W = jax.random.normal(k3, (F_in, F_out), dtype=jnp.float32) * (1.0 / np.sqrt(F_in))
        a = jax.random.normal(k4, (2 * F_out, 1), dtype=jnp.float32) * (1.0 / np.sqrt(2 * F_out))
        return {'x': x, 'adj': adj, 'W': W, 'a': a}
    _L3_gnn_all = _L3_gnn_setup()
    _L3_gnn_in = {k: v for k, v in _L3_gnn_all.items() if k in ('W', 'a')}
    del _L3_gnn_all
    return {'x': x, 'adj': adj, 'L0_gnn_attn': _L0_gnn_in['attn'], 'L3_gnn_W': _L3_gnn_in['W'], 'L3_gnn_a': _L3_gnn_in['a']}

def reference(x, adj, L0_gnn_attn, L3_gnn_W, L3_gnn_a):
    import jax
    import jax.numpy as jnp

    def _L0_gnn_ref(adj, emb, attn):
        import jax, jax.numpy as jnp
        import numpy as np
        N, D = (4096, 128)
        d = emb.shape[1]
        s_i = emb @ attn[:d]
        s_j = emb @ attn[d:]
        e = jax.nn.leaky_relu(s_i + s_j.T, negative_slope=0.2)
        neg_inf = jnp.float32(-1000000000.0)
        e = e + jnp.where(adj > 0, jnp.float32(0.0), neg_inf)
        alpha = jax.nn.softmax(e, axis=1)
        return alpha @ emb

    def _L1_gnn_ref(X, adj):
        import jax
        import jax.numpy as jnp
        import numpy as np
        from jax import lax
        N = 4096
        F = 128
        CHUNK = 64
        neg = jnp.finfo(X.dtype).min
        mask = adj != 0
        n, f = X.shape

        def body(_, mrows):
            vals = jnp.max(jnp.where(mrows[:, :, None], X[None, :, :], neg), axis=1)
            has_nbr = jnp.any(mrows, axis=1)
            return (None, jnp.where(has_nbr[:, None], vals, jnp.zeros((), X.dtype)))
        _, out = lax.scan(body, None, mask.reshape(n // CHUNK, CHUNK, n))
        return out.reshape(n, f)

    def _L2_gnn_ref(x, adj):
        import jax, jax.numpy as jnp
        import numpy as np
        from jax import lax
        N = 4096
        D = 128
        CHUNK = 128
        n, d = x.shape
        neg = jnp.finfo(x.dtype).min
        adj_chunks = adj.reshape(n // CHUNK, CHUNK, n)

        def step(carry, a):
            mask = a != 0
            masked = jnp.where(mask[:, :, None], x[None, :, :], neg)
            m = jnp.max(masked, axis=1)
            has_nbr = jnp.any(mask, axis=1)
            out = jnp.where(has_nbr[:, None], m, jnp.zeros((), x.dtype))
            return (carry, out)
        _, out = lax.scan(step, None, adj_chunks)
        return out.reshape(n, d)

    def _L3_gnn_ref(x, adj, W, a):
        import jax, jax.numpy as jnp
        import numpy as np
        NEG_INF = -9000000000000000.0
        ALPHA = 0.2
        h = x @ W
        F_out = h.shape[1]
        a_src = a[:F_out, 0]
        a_dst = a[F_out:, 0]
        s_src = h @ a_src
        s_dst = h @ a_dst
        e = jax.nn.leaky_relu(s_src[:, None] + s_dst[None, :], negative_slope=ALPHA)
        e = jnp.where(adj > 0, e, jnp.float32(NEG_INF))
        attention = jax.nn.softmax(e, axis=1)
        h_prime = attention @ h
        return h_prime
    x = _layernorm(x + _L0_gnn_ref(adj, x, L0_gnn_attn), axis=-1)
    x = _layernorm(x + _L1_gnn_ref(x, adj), axis=-1)
    x = _layernorm(x + _L2_gnn_ref(x, adj), axis=-1)
    x = _layernorm(x + _L3_gnn_ref(x, adj, L3_gnn_W, L3_gnn_a), axis=-1)
    return x

_drawn_inputs = setup_inputs


def setup_inputs(seed=0):
    import zlib

    import numpy as np

    out = dict(_drawn_inputs(seed))
    spreads = {}
    factors = {}
    for name, (base, spread) in spreads.items():
        noise = np.random.default_rng([zlib.crc32(name.encode()), seed]).standard_normal(out[name].shape)
        drawn = base * np.exp(spread * noise) if base else spread * noise
        out[name] = jnp.asarray(drawn.astype(out[name].dtype))
    for name, factor in factors.items():
        out[name] = (out[name] * factor).astype(out[name].dtype)
    return out
```

```python
from contextlib import ExitStack

import concourse.bass as bass
from concourse import mybir

ALU = mybir.AluOpType
ACT = mybir.ActivationFunctionType
AX = mybir.AxisListType
F32 = mybir.dt.float32
BF16 = mybir.dt.bfloat16
I32 = mybir.dt.int32
U32 = mybir.dt.uint32
U16 = mybir.dt.uint16

P = 128
F = 128
N = 4096
T = N // P
SLOTS = 16
QUARTER = N // 4
EPS = 1e-5
SLOPE = 0.2
MASKED = -1e9
LOWEST = -3.4028234663852886e38
FAR = -1e30

SERVED = [32, 30, 26, 20, 13, 8, 5, 3] + [1] * 8
DEPTH = [sum(n > t for n in SERVED) for t in range(T)]
GATHERS = sum(DEPTH)
GROUPS = []
for _t in range(T):
    if GROUPS and GROUPS[-1][2] == DEPTH[_t]:
        GROUPS[-1][1] += 1
    else:
        GROUPS.append([_t, 1, DEPTH[_t], sum(DEPTH[:_t])])
LEVELS = SLOTS + 2

STEPS = {0: 15, 1: 7, 2: 7, 3: 16}

C_SDST, C_RANK, C_SSRC, C_DEG, C_NBR, C_ID = F, F + 1, F + 2, F + 3, F + 4, F + 4 + SLOTS
RECORD = C_ID + 1
W0 = F + 4
W3 = F + 2


def gnn_kernel(nc, x, adj, attn, w, a3, out):
    with ExitStack() as ctx:
        def sb(name, shape, dt):
            return ctx.enter_context(nc.sbuf_tensor(name, shape, dt))

        def ps(name, shape, dt=F32):
            return ctx.enter_context(nc.psum_tensor(name, shape, dt))

        def sem(name):
            return ctx.enter_context(nc.semaphore(name))

        table0 = nc.dram_tensor("table0", [N + 1, W0], F32).ap()
        table1 = nc.dram_tensor("table1", [N + 1, F], F32).ap()
        table2 = nc.dram_tensor("table2", [N + 1, F], F32).ap()
        table3 = nc.dram_tensor("table3", [N + 1, W3], F32).ap()
        ranked_dram = nc.dram_tensor("ranked_dram", [N, RECORD], F32).ap()
        dense_dram = [nc.dram_tensor(f"dense_dram{i}", [N, F], F32).ap() for i in range(3)]
        dst_dram = {i: nc.dram_tensor(f"dst_dram{i}", [N], F32).ap() for i in (0, 3)}

        work = sb("work", [P, GATHERS * W0], F32)
        adj_buf = [work[:, b * N:(b + 1) * N].bitcast(I32) for b in range(2)]
        mask_buf = [work[:, 2 * N + b * (N // 2):2 * N + (b + 1) * (N // 2)].bitcast(BF16) for b in range(2)]
        key_buf = [work[:, 3 * N + b * (N // 2):3 * N + (b + 1) * (N // 2)].bitcast(U16) for b in range(2)]
        column_no = sb("column_no", [P, N], U16)
        record = sb("record", [P, T, RECORD], F32)
        record_i = record[:, :, :].bitcast(I32)
        ranked = sb("ranked", [P, T, RECORD], F32)
        ranked_i = ranked[:, :, :].bitcast(I32)
        big = sb("big", [P, 2, T * (F + 4)], F32)
        weights_t = big[:, 0, 0:T * F].rearrange("p (t i) -> p t i", t=T)
        h = big[:, 1, 0:T * W3].rearrange("p (t f) -> p t f", t=T)
        ident = sb("ident", [P, P], F32)
        ones = sb("ones", [P, P], F32)
        attn_cols = sb("attn_cols", [P, 2], F32)
        a3_cols = sb("a3_cols", [P, 2], F32)
        w_aug = sb("w_aug", [P, W3], F32)
        w_t = sb("w_t", [P, F], F32)
        x_t = sb("x_t", [P, 2, 4 * P], F32)
        empty = sb("empty", [1, 4, W0], F32)
        found = sb("found", [P, 2, 32], F32)
        found2 = sb("found2", [P, 2, 32], F32)
        top16 = sb("top16", [P, 2, SLOTS], F32)
        held_word = sb("held_word", [P, 5], F32)
        row_sum = sb("row_sum", [P, T], F32)
        low_bf = sb("low_bf", [P, P], BF16)
        ones_bf = sb("ones_bf", [P, P], BF16)
        held = sb("held", [P, T, SLOTS], F32)
        small = sb("small", [P, 4, T], F32)
        level_of = sb("level_of", [P, LEVELS, T], F32)
        onehot = sb("onehot", [P, LEVELS, T], BF16)
        PAD = 16
        pre = [sb(f"pre{b}", [P, LEVELS, PAD + T], F32) for b in range(2)]
        lev = [sb(f"lev{b}", [P, PAD + LEVELS], F32) for b in range(2)]
        place = sb("place", [P, LEVELS, T], F32)
        total = sb("total", [P, LEVELS, T], F32)
        rank_i = sb("rank_i", [P, T], I32)
        caps = sb("caps", [P, LEVELS - 1], F32)
        over = sb("over", [P, LEVELS], F32)
        flag_f = sb("flag_f", [P, 1], F32)
        flag_i = sb("flag_i", [P, 1], I32)
        nbr_rank = sb("nbr_rank", [P, GATHERS], I32)
        maxn = max(n for _, n, _, _ in GROUPS)
        maxs = max(n * k for _, n, k, _ in GROUPS)
        score = sb("score", [P, 2, maxs], F32)
        stat = sb("stat", [P, 8, maxn], F32)
        y = sb("y", [P, maxn, F], F32)
        moments = sb("moments", [P, maxn, 6], F32)
        mean_var = sb("mean_var", [P, maxn, 2], F32)
        has_nbr = sb("has_nbr", [P, T], F32)
        no_nbr = sb("no_nbr", [P, T], F32)
        best_dst = sb("best_dst", [P, 2], F32)
        diag = sb("diag", [P, P], F32)
        row_max = sb("row_max", [P, 2, P], F32)
        lone = sb("lone", [P, F], F32)
        lone_sum = sb("lone_sum", [P, 1], F32)
        h_mean = sb("h_mean", [P, F], F32)
        x3_t = sb("x3_t", [P, 2, P], F32)
        mean_w = sb("mean_w", [P, P], F32)

        d_adj = [work[:, b * N:(b + 1) * N].bitcast(I32) for b in range(2)]
        d_e = work[:, 2 * N:3 * N]
        d_m = work[:, 3 * N:4 * N]
        d_dst = big[:, 0, 0:N]
        d_xt = big[:, 0, 0:N]
        d_pt = big[:, 1, 0:N]
        d_max_t = big[:, 1, 0:N]
        d_has = ranked[:, :, :].rearrange("p t r -> p (t r)")[:, 0:N]
        d_y = sb("d_y", [P, 2, F], F32)
        d_own = sb("d_own", [P, F], F32)
        d_col = sb("d_col", [P, 8], F32)
        d_mom = sb("d_mom", [P, 6], F32)
        d_mv = sb("d_mv", [P, 2], F32)

        ps_tr = [ps(f"ps_tr{b}", [P, 512]) for b in range(2)]
        ps_mm = [ps(f"ps_mm{b}", [P, 512]) for b in range(2)]
        ps_small = ps("ps_small", [P, 512])
        ps_acc = ps("ps_acc", [P, 512])
        ps_lt = [ps_tr[0], ps_tr[1]]
        ps_tot = [ps_mm[0], ps_mm[1]]

        adj_loaded = [sem(f"adj_loaded{b}") for b in range(2)]
        masked = sem("masked")
        keyed = sem("keyed")
        searched = sem("searched")
        params_loaded = sem("params_loaded")
        x_loaded = sem("x_loaded")
        pool_made = sem("pool_made")
        x_transposed = sem("x_transposed")
        xt_copied = sem("xt_copied")
        scored = sem("scored")
        score_copied = sem("score_copied")
        w_turned = sem("w_turned")
        wt_copied = sem("wt_copied")
        wa_made = sem("wa_made")
        wa_copied = sem("wa_copied")
        dve_step = sem("dve_step")
        onehot_made = sem("onehot_made")
        counted = sem("counted")
        ranks_made = sem("ranks_made")
        flag_made = sem("flag_made")
        tops_made = sem("tops_made")
        best_made = sem("best_made")
        empty_written = sem("empty_written")
        table0_written = sem("table0_written")
        scattered = sem("scattered")
        lists_loaded = sem("lists_loaded")
        x_ranked = sem("x_ranked")
        gathered = [sem(f"gathered{g}") for g in range(len(GROUPS))]
        scores_ready = sem("scores_ready")
        exps_ready = sem("exps_ready")
        variance_ready = sem("variance_ready")
        deviation_ready = sem("deviation_ready")
        diag_made = sem("diag_made")
        src_spread = sem("src_spread")
        lone_scored = sem("lone_scored")
        lone_exp = sem("lone_exp")
        lone_summed = sem("lone_summed")
        layer_done = [sem(f"layer{i}_done") for i in range(4)]
        table_written = {i: sem(f"table{i}_written") for i in (1, 2, 3)}
        x3_turned = sem("x3_turned")
        x3t_copied = sem("x3t_copied")
        h_made = sem("h_made")
        h_copied = sem("h_copied")
        mean_made = sem("mean_made")
        out_written = sem("out_written")
        DENSE = {}
        for layer in range(4):
            names = ["x_in", "step", "dev", "var", "stored"]
            if layer in (0, 3):
                names += ["v_ready", "dst_out", "dst_in", "adj", "score", "exp", "turned", "copied", "acc"]
            if layer == 3:
                names += ["x_turned", "x_copied", "h_made"]
            if layer in (1, 2):
                names += ["x_turned", "x_copied", "row_even", "row_odd", "row_read", "row_step", "maxed", "back"]
            DENSE[layer] = {k: sem(f"dense{layer}_{k}") for k in names}

        block = ctx.enter_context(nc.Block())

        def gat(width, slot, count):
            return work[:, slot * width:(slot + count) * width]

        @block.sync
        def _(sp):
            for t in range(2):
                sp.dma_start(adj_buf[t], adj[t * P:(t + 1) * P, :]).then_inc(adj_loaded[t], 16)
            with sp.Fori(0, T // 2 - 1) as pair:
                for b in range(2):
                    sp.wait_ge(masked, pair * 2 + (b + 1))
                    sp.dma_start(adj_buf[b], adj[bass.ds(pair * (2 * P) + (2 + b) * P, P), :]).then_inc(adj_loaded[b], 16)
            sp.wait_ge(ranks_made, 2)
            sp.wait_ge(score_copied, T // 4)
            sp.wait_ge(x_loaded, 16)
            sp.dma_start(table0[1:N + 1, :].rearrange("(t p) f -> p t f", p=P),
                         record[:, :, 0:W0]).then_inc(table0_written, 16)
            sp.wait_ge(flag_made, 1)
            big_degree = sp.value_load(flag_i[0:1, 0:1], min_val=0, max_val=64)
            with sp.If(big_degree == 0):
                sp.wait_ge(scattered, 16 * T)
                sp.dma_start(ranked[:, :, C_SDST:RECORD],
                             ranked_dram.rearrange("(t p) f -> p t f", p=P)[:, :, C_SDST:RECORD]).then_inc(lists_loaded, 16)
                for layer, table, width in ((1, table1, F), (2, table2, F)):
                    for g, (t0, n, _, _) in enumerate(GROUPS):
                        sp.wait_ge(layer_done[layer - 1], g + 1)
                        sp.dma_start(table[1 + t0 * P:1 + (t0 + n) * P, :].rearrange("(t p) f -> p t f", p=P),
                                     ranked[:, t0:t0 + n, 0:F]).then_inc(table_written[layer], 16)
                for g, (t0, n, _, _) in enumerate(GROUPS):
                    sp.wait_ge(h_copied, t0 + n)
                    sp.dma_start(table3[1 + t0 * P:1 + (t0 + n) * P, :].rearrange("(t p) f -> p t f", p=P),
                                 h[:, t0:t0 + n, :]).then_inc(table_written[3], 16)
            with sp.Else():
                for layer in range(4):
                    d = DENSE[layer]
                    to = out if layer == 3 else dense_dram[layer]
                    if layer:
                        sp.wait_ge(DENSE[layer - 1]["stored"], 16 * T)
                        sp.dma_start(record[:, :, 0:F], dense_dram[layer - 1].rearrange("(t p) f -> p t f", p=P)).then_inc(d["x_in"], 16)
                    if layer in (0, 3):
                        sp.wait_ge(d["v_ready"], 1 if layer == 0 else T)
                        sp.dma_start(dst_dram[layer].rearrange("(t p) -> p t", p=P), ranked[:, :, C_SDST],
                                     allow_slow_non_contiguous=True).then_inc(d["dst_out"], 16)
                        sp.wait_ge(d["dst_out"], 16)
                        sp.dma_start(d_dst, dst_dram[layer].partition_broadcast(P)).then_inc(d["dst_in"], 16)
                        with sp.Fori(0, T) as t:
                            sp.dma_start(d_adj[0], adj[bass.ds(t * P, P), :]).then_inc(d["adj"], 16)
                            sp.wait_ge(d["step"], t * STEPS[layer] + STEPS[layer])
                            sp.dma_start(to[bass.ds(t * P, P), :], d_y[:, 1, :]).then_inc(d["stored"], 16)
                    else:
                        rows = (d["row_even"], d["row_odd"])
                        for b in range(2):
                            sp.dma_start(d_adj[b], adj[b, :].partition_broadcast(P)).then_inc(rows[b], 16)
                        with sp.Fori(0, N // 2 - 1) as pair:
                            for b in range(2):
                                sp.wait_ge(d["row_read"], pair * 2 + (b + 1))
                                sp.dma_start(d_adj[b], adj[bass.ds(pair * 2 + (2 + b), 1), :].rearrange("a n -> (a n)").partition_broadcast(P)).then_inc(rows[b], 16)
                        with sp.Fori(0, T) as t:
                            sp.wait_ge(d["step"], t * STEPS[layer] + STEPS[layer])
                            sp.dma_start(to[bass.ds(t * P, P), :], d_y[:, 1, :]).then_inc(d["stored"], 16)
                sp.wait_ge(DENSE[3]["stored"], 16 * T)

        @block.gpsimd
        def _(pool):
            made = 0

            def make(ins):
                nonlocal made
                made += 1
                ins.then_inc(pool_made, 1)
                return made

            make(nc.gpsimd.iota(column_no[:, :], pattern=[[1, N]], base=1, channel_multiplier=0,
                                allow_small_or_imprecise_dtypes=True))
            make(nc.gpsimd.memset(ones[:, :], 1.0))
            pool.wait_ge(pool_made, made)
            make(nc.gpsimd.affine_select(out=ident[:, :], in_=ones[:, :], pattern=[[1, P]],
                                         compare_op=ALU.is_equal, fill=0.0, base=0, channel_multiplier=-1))
            make(nc.gpsimd.memset(ones_bf[:, :], 1.0))
            pool.wait_ge(pool_made, made)
            make(nc.gpsimd.affine_select(out=low_bf[:, :], in_=ones_bf[:, :], pattern=[[1, P]],
                                         compare_op=ALU.is_gt, fill=0.0, base=0, channel_multiplier=-1))
            make(nc.gpsimd.iota(level_of[:, :, :], pattern=[[-1, LEVELS], [0, T]], base=LEVELS - 1,
                                channel_multiplier=0, allow_small_or_imprecise_dtypes=True))
            make(nc.gpsimd.iota(record_i[:, :, C_ID], pattern=[[P, T]], base=0, channel_multiplier=1))
            make(nc.gpsimd.memset(mean_w[:, :], 1.0 / N))
            make(nc.gpsimd.memset(empty[:, :, :], 0.0))
            pool.wait_ge(pool_made, made)
            make(nc.gpsimd.memset(empty[:, 0, C_SDST:C_SDST + 1], FAR))
            make(nc.gpsimd.memset(empty[:, 1, :], LOWEST))
            make(nc.gpsimd.memset(empty[:, 3, C_SDST:C_SDST + 1], FAR))
            make(nc.gpsimd.memset(caps[:, 0:1], 0.0))
            for level in range(1, LEVELS - 1):
                make(nc.gpsimd.memset(caps[:, level:level + 1], float(P * SERVED[SLOTS - level])))
            pool.wait_ge(tops_made, 1)
            nc.gpsimd.partition_all_reduce(best_dst[:, 1:2], best_dst[:, 0:1], P,
                                           bass.bass_isa.ReduceOp.max).then_inc(best_made, 1)
            pool.wait_ge(flag_made, 1)
            big_degree = pool.value_load(flag_i[0:1, 0:1], min_val=0, max_val=64)
            with pool.If(big_degree == 0):
                pool.wait_ge(ranks_made, 2)
                pool.wait_ge(score_copied, T // 4)
                pool.wait_ge(x_loaded, 16)
                for t in range(T):
                    pool.indirect_dma_start(out=ranked_dram, out_offset=bass.IndirectOffsetOnAxis(ap=rank_i[:, t:t + 1], axis=0),
                                            in_=record[:, t, :], in_offset=None).then_inc(scattered, 16)
                pool.wait_ge(lists_loaded, 16)
                pool.wait_ge(table0_written, 16)
                pool.wait_ge(empty_written, 16 * 4)

                def gather(table, width, index):
                    for g, (t0, n, depth, s0) in enumerate(GROUPS):
                        for t in range(t0, t0 + n):
                            for k in range(depth):
                                s = s0 + (t - t0) * depth + k
                                pool.indirect_dma_start(
                                    out=gat(width, s, 1), out_offset=None, in_=table,
                                    in_offset=bass.IndirectOffsetOnAxis(ap=index(t, s, k), axis=0),
                                ).then_inc(gathered[g], 16)

                gather(table0, W0, lambda t, s, k: ranked_i[:, t, C_NBR + k:C_NBR + k + 1])
                for layer, table, width in ((1, table1, F), (2, table2, F), (3, table3, W3)):
                    pool.wait_ge(layer_done[layer - 1], len(GROUPS))
                    pool.wait_ge(table_written[layer], 16 * len(GROUPS))
                    gather(table, width, lambda t, s, k: nbr_rank[:, s:s + 1])
                for g, (t0, n, _, _) in enumerate(GROUPS):
                    pool.wait_ge(layer_done[3], g + 1)
                    for t in range(t0, t0 + n):
                        pool.indirect_dma_start(out=out, out_offset=bass.IndirectOffsetOnAxis(ap=ranked_i[:, t, C_ID:C_ID + 1], axis=0),
                                                in_=ranked[:, t, 0:F], in_offset=None).then_inc(out_written, 16)
                pool.wait_ge(out_written, 16 * T)

        @block.scalar
        def _(act):
            act.dma_start(attn_cols[:, :], attn.rearrange("(c f) o -> f (c o)", f=F), allow_slow_non_contiguous=True).then_inc(params_loaded, 16)
            act.dma_start(a3_cols[:, :], a3.rearrange("(c f) o -> f (c o)", f=F), allow_slow_non_contiguous=True).then_inc(params_loaded, 16)
            act.dma_start(w_aug[:, 0:F], w).then_inc(params_loaded, 16)
            act.dma_start(record[:, :, 0:F], x.rearrange("(t p) f -> p t f", p=P)).then_inc(x_loaded, 16)
            act.wait_ge(pool_made, 12)
            act.dma_start(table0[0:1, :], empty[:, 0, :]).then_inc(empty_written, 16)
            act.dma_start(table1[0:1, :], empty[:, 1, 0:F]).then_inc(empty_written, 16)
            act.dma_start(table2[0:1, :], empty[:, 1, 0:F]).then_inc(empty_written, 16)
            act.dma_start(table3[0:1, :], empty[:, 3, 0:W3]).then_inc(empty_written, 16)

            def mask(t, b, turn):
                act.wait_ge(adj_loaded[b], turn)
                nc.scalar.activation(mask_buf[b], adj_buf[b].bitcast(U32), ACT.Copy,
                                     accum_out=row_sum[:, bass.ds(t, 1)]).then_inc(masked, 1)

            mask(0, 0, 16)
            mask(1, 1, 16)
            for q in range(T // 4):
                act.wait_ge(x_transposed, q + 1)
                if q >= 2:
                    act.wait_ge(scored, q - 1)
                nc.scalar.copy(x_t[:, q % 2, :], ps_tr[q % 2][:, :]).then_inc(xt_copied, 1)
                act.wait_ge(scored, q + 1)
                src = ps_small[:, 8 * q:8 * q + 8].rearrange("p (t c) -> p t c", c=2)
                nc.scalar.copy(record[:, 4 * q:4 * q + 4, C_SSRC], src[:, :, 0])
                nc.scalar.copy(record[:, 4 * q:4 * q + 4, C_SDST], src[:, :, 1]).then_inc(score_copied, 1)
            act.wait_ge(w_turned, 1)
            nc.scalar.copy(w_t[:, :], ps_mm[0][:, 0:F]).then_inc(wt_copied, 1)
            act.wait_ge(wa_made, 1)
            nc.scalar.copy(w_aug[:, F:F + 1], ps_mm[1][:, 1:2])
            nc.scalar.copy(w_aug[:, F + 1:F + 2], ps_mm[1][:, 0:1]).then_inc(wa_copied, 1)
            with act.Fori(0, T // 2 - 1) as pair:
                for b in range(2):
                    act.wait_ge(keyed, pair * 2 + (b + 1))
                    mask(pair * 2 + (b + 2), b, pair * 16 + 32)
            act.wait_ge(flag_made, 1)
            big_degree = act.value_load(flag_i[0:1, 0:1], min_val=0, max_val=64)
            with act.If(big_degree == 0):
                act.wait_ge(scattered, 16 * T)
                act.dma_start(ranked[:, :, 0:C_SDST],
                              ranked_dram.rearrange("(t p) f -> p t f", p=P)[:, :, 0:C_SDST]).then_inc(x_ranked, 16)

                G = len(GROUPS)

                def exponential(g, first):
                    _, n, depth, _ = GROUPS[g]
                    act.wait_ge(scores_ready, first + g + 1)
                    nc.scalar.activation(score[:, g % 2, 0:n * depth], score[:, g % 2, 0:n * depth],
                                         ACT.Exp).then_inc(exps_ready, 1)

                def root(g, layer):
                    n = GROUPS[g][1]
                    act.wait_ge(variance_ready, layer * G + g + 1)
                    nc.scalar.activation(stat[:, 6, 0:n], stat[:, 5, 0:n], ACT.Sqrt).then_inc(deviation_ready, 1)

                def attention(first, layer):
                    exponential(0, first)
                    for g in range(G):
                        if g + 1 < G:
                            exponential(g + 1, first)
                        root(g, layer)

                act.wait_ge(lone_scored, 1)
                nc.scalar.activation(big[:, 0, 0:T * F], big[:, 0, 0:T * F], ACT.Exp).then_inc(lone_exp, 1)
                attention(0, 0)
                for layer in (1,):
                    for g in range(G):
                        root(g, layer)
                for g in range(G + 1):
                    if g < G:
                        root(g, 2)
                    if g >= 1:
                        t0, n, _, _ = GROUPS[g - 1]
                        for t in range(t0, t0 + n):
                            act.wait_ge(x3_turned, t + 1)
                            if t >= 2:
                                act.wait_ge(h_made, t - 1)
                            nc.scalar.copy(x3_t[:, t % 2, :], ps_tr[t % 2][:, 0:P]).then_inc(x3t_copied, 1)
                            act.wait_ge(h_made, t + 1)
                            nc.scalar.copy(h[:, t, :], ps_mm[t % 2][:, 0:W3]).then_inc(h_copied, 1)
                attention(G, 3)
            with act.Else():
                for layer in range(4):
                    d = DENSE[layer]
                    if layer == 3:
                        with act.Fori(0, T) as t:
                            act.wait_ge(d["x_turned"], t + 1)
                            nc.scalar.copy(x3_t[:, 0, :], ps_tr[0][:, 0:P]).then_inc(d["x_copied"], 1)
                            act.wait_ge(d["h_made"], t + 1)
                            nc.scalar.copy(ranked[:, bass.ds(t, 1), 0:F + 1], ps_mm[0][:, 0:F + 1].unsqueeze(1))
                            nc.scalar.copy(ranked[:, bass.ds(t, 1), C_SSRC], ps_mm[0][:, F + 1:F + 2]).then_inc(d["v_ready"], 1)
                    if layer in (0, 3):
                        with act.Fori(0, T) as t:
                            act.wait_ge(d["score"], t + 1)
                            nc.scalar.activation(d_e, d_e, ACT.Exp, bias=d_col[:, 1:2], accum_out=d_col[:, 2:3]).then_inc(d["exp"], 1)
                            for q in range(T // 4):
                                act.wait_ge(d["turned"], t * (T // 4) + (q + 1))
                                nc.scalar.copy(d_pt[:, q * 4 * P:(q + 1) * 4 * P], ps_tr[q % 2][:, :]).then_inc(d["copied"], 1)
                            act.wait_ge(d["var"], t + 1)
                            nc.scalar.activation(d_col[:, 4:5], d_col[:, 3:4], ACT.Sqrt).then_inc(d["dev"], 1)
                    else:
                        for q in range(T // 4):
                            act.wait_ge(d["x_turned"], q + 1)
                            nc.scalar.copy(d_xt[:, q * 4 * P:(q + 1) * 4 * P], ps_tr[q % 2][:, :]).then_inc(d["x_copied"], 1)
                        with act.Fori(0, T) as t:
                            act.wait_ge(d["var"], t + 1)
                            nc.scalar.activation(d_col[:, 4:5], d_col[:, 3:4], ACT.Sqrt).then_inc(d["dev"], 1)

        @block.tensor
        def _(pe):
            pe.wait_ge(x_loaded, 16)
            pe.wait_ge(pool_made, 3)
            pe.wait_ge(params_loaded, 48)
            for q in range(T // 4):
                if q >= 2:
                    pe.wait_ge(xt_copied, q - 1)
                for j in range(4):
                    last = nc.tensor.transpose(ps_tr[q % 2][:, j * P:(j + 1) * P], record[:, 4 * q + j, 0:F], ident[:, :])
                last.then_inc(x_transposed, 1)
                pe.wait_ge(xt_copied, q + 1)
                for j in range(4):
                    last = nc.tensor.matmul(ps_small[:, 8 * q + 2 * j:8 * q + 2 * j + 2], x_t[:, q % 2, j * P:(j + 1) * P],
                                            attn_cols[:, :], start=True, stop=True)
                last.then_inc(scored, 1)
            nc.tensor.transpose(ps_mm[0][:, 0:F], w_aug[:, 0:F], ident[:, :]).then_inc(w_turned, 1)
            pe.wait_ge(wt_copied, 1)
            nc.tensor.matmul(ps_mm[1][:, 0:2], w_t[:, :], a3_cols[:, :], start=True, stop=True).then_inc(wa_made, 1)
            pe.wait_ge(onehot_made, 1)
            pe.wait_ge(wa_copied, 1)
            pe.wait_ge(xt_copied, T // 4)
            pe.wait_ge(pool_made, 5)
            half = LEVELS // 2
            for b in range(2):
                ohb = onehot[:, b * half:(b + 1) * half, :].rearrange("p l t -> p (l t)")
                nc.tensor.matmul(ps_lt[b][:, 0:half * T], low_bf[:, :], ohb, start=True, stop=True)
                last = nc.tensor.matmul(ps_tot[b][:, 0:half * T], ones_bf[:, :], ohb, start=True, stop=True)
            last.then_inc(counted, 1)
            pe.wait_ge(flag_made, 1)
            big_degree = pe.value_load(flag_i[0:1, 0:1], min_val=0, max_val=64)
            with pe.If(big_degree == 0):
                pe.wait_ge(diag_made, 1)
                nc.tensor.matmul(ps_small[:, 128:256], ones[:, :], diag[:, :], start=True, stop=True).then_inc(src_spread, 1)
                pe.wait_ge(lone_exp, 1)
                for t in range(T):
                    nc.tensor.matmul(ps_acc[:, 0:F], weights_t[:, t, :], record[:, t, 0:F], start=(t == 0), stop=(t == T - 1))
                for t in range(T):
                    last = nc.tensor.matmul(ps_small[:, 256:257], weights_t[:, t, :], ones[:, 0:1], start=(t == 0), stop=(t == T - 1))
                last.then_inc(lone_summed, 1)
                def mean(t):
                    pe.wait_ge(h_copied, t + 1)
                    return nc.tensor.matmul(ps_acc[:, 128:128 + F], mean_w[:, :], h[:, t, 0:F], start=(t == 0), stop=(t == T - 1))

                for g, (t0, n, _, _) in enumerate(GROUPS):
                    pe.wait_ge(layer_done[2], g + 1)
                    for t in range(t0, t0 + n):
                        if t >= 2:
                            pe.wait_ge(x3t_copied, t - 1)
                        nc.tensor.transpose(ps_tr[t % 2][:, 0:P], ranked[:, t, 0:F], ident[:, :]).then_inc(x3_turned, 1)
                        pe.wait_ge(x3t_copied, t + 1)
                        if t >= 2:
                            pe.wait_ge(h_copied, t - 1)
                        nc.tensor.matmul(ps_mm[t % 2][:, 0:W3], x3_t[:, t % 2, :], w_aug[:, :], start=True, stop=True).then_inc(h_made, 1)
                        if t >= 1:
                            mean(t - 1)
                mean(T - 1).then_inc(mean_made, 1)
            with pe.Else():
                for layer in range(4):
                    d = DENSE[layer]
                    if layer:
                        pe.wait_ge(d["x_in"], 16)
                    if layer == 3:
                        for t in range(T):
                            nc.tensor.transpose(ps_tr[0][:, 0:P], record[:, t, 0:F], ident[:, :]).then_inc(d["x_turned"], 1)
                            pe.wait_ge(d["x_copied"], t + 1)
                            nc.tensor.matmul(ps_mm[0][:, 0:W3], x3_t[:, 0, :], w_aug[:, :], start=True, stop=True).then_inc(d["h_made"], 1)
                            pe.wait_ge(d["v_ready"], t + 1)
                    if layer in (0, 3):
                        with pe.Fori(0, T) as t:
                            pe.wait_ge(d["exp"], t + 1)
                            for q in range(T // 4):
                                if q >= 2:
                                    pe.wait_ge(d["copied"], t * (T // 4) + (q - 1))
                                for j in range(4):
                                    c = (4 * q + j) * P
                                    last = nc.tensor.transpose(ps_tr[q % 2][:, j * P:(j + 1) * P], d_e[:, c:c + P], ident[:, :])
                                last.then_inc(d["turned"], 1)
                            pe.wait_ge(d["copied"], t * (T // 4) + T // 4)
                            for j in range(T):
                                last = nc.tensor.matmul(ps_acc[:, 0:F], d_pt[:, j * P:(j + 1) * P], ranked[:, j, 0:F], start=(j == 0), stop=(j == T - 1))
                            last.then_inc(d["acc"], 1)
                            pe.wait_ge(d["step"], t * STEPS[layer] + STEPS[layer])
                    else:
                        for q in range(T // 4):
                            if q >= 2:
                                pe.wait_ge(d["x_copied"], q - 1)
                            for j in range(4):
                                last = nc.tensor.transpose(ps_tr[q % 2][:, j * P:(j + 1) * P], record[:, 4 * q + j, 0:F], ident[:, :])
                            last.then_inc(d["x_turned"], 1)
                        pe.wait_ge(d["maxed"], 1)
                        for t in range(T):
                            nc.tensor.transpose(ps_mm[0][:, 0:P], d_max_t[:, t * P:(t + 1) * P], ident[:, :]).then_inc(d["back"], 1)
                            pe.wait_ge(d["step"], t * STEPS[layer] + STEPS[layer])

        @block.vector
        def _(dve):
            V = nc.vector
            steps = 0

            def do(ins):
                nonlocal steps
                steps += 1
                ins.then_inc(dve_step, 1)
                return steps

            def after(n=None):
                dve.wait_ge(dve_step, steps if n is None else n)

            for b in range(2):
                do(V.memset(pre[b][:, :, :], 0.0))
                do(V.memset(lev[b][:, :], 0.0))
            dve.wait_ge(pool_made, 1)
            def hold(i, ap):
                V.tensor_copy(held_word[:, i:i + 1], ap)

            with dve.Fori(0, T // 2) as pair:
                for b in range(2):
                    dve.wait_ge(masked, pair * 2 + (b + 1))
                    V.tensor_tensor(key_buf[b], mask_buf[b], column_no[:, :], ALU.mult).then_inc(keyed, 1)
                for b in range(2):
                    dve.wait_ge(keyed, pair * 2 + (b + 1))
                    hold(b, key_buf[b][:, 0:1])
                    for q in range(4):
                        last = V.max(found[:, b, 8 * q:8 * q + 8], key_buf[b][:, q * QUARTER:(q + 1) * QUARTER])
                last.then_inc(searched, 1)
                dve.wait_ge(searched, pair * 4 + 1)
                hold(2, found[:, 0, 0:1])
                V.max(top16[:, 0, 0:8], found[:, 0, :])
                V.max(top16[:, 1, 0:8], found[:, 1, :]).then_inc(searched, 1)
                dve.wait_ge(searched, pair * 4 + 2)
                hold(3, top16[:, 0, 0:1])
                V.match_replace(found2[:, 0, :], top16[:, 0, 0:8], found[:, 0, :], 0.0)
                V.match_replace(found2[:, 1, :], top16[:, 1, 0:8], found[:, 1, :], 0.0).then_inc(searched, 1)
                dve.wait_ge(searched, pair * 4 + 3)
                hold(4, found2[:, 0, 0:1])
                V.max(top16[:, 0, 8:16], found2[:, 0, :])
                V.max(top16[:, 1, 8:16], found2[:, 1, :]).then_inc(searched, 1)
                dve.wait_ge(searched, pair * 4 + 4)
                V.tensor_copy(record_i[:, bass.ds(pair * 2, 2), C_NBR:C_NBR + SLOTS], top16[:, :, :]).then_inc(dve_step, 1)
            steps += T // 2
            after()
            do(V.tensor_single_scalar(held[:, :, :], record_i[:, :, C_NBR:C_NBR + SLOTS], 0.0, op=ALU.is_gt)); after()
            deg = record[:, :, C_DEG]
            do(V.tensor_reduce(deg, held[:, :, :], AX.X, ALU.add)); after()
            dve.wait_ge(masked, T)
            do(V.tensor_tensor(small[:, 0, :], row_sum[:, :], deg, ALU.is_equal)); after()
            do(V.scalar_tensor_tensor(small[:, 1, :], deg, float(-(SLOTS + 1)), small[:, 0, :], ALU.add, ALU.mult)); after()
            do(V.tensor_scalar_add(small[:, 2, :], small[:, 1, :], float(SLOTS + 1))); after()
            dve.wait_ge(pool_made, 6)
            V.tensor_tensor(onehot[:, :, :], level_of[:, :, :], small[:, 2, :].unsqueeze(1).to_broadcast([P, LEVELS, T]),
                            ALU.is_equal).then_inc(onehot_made, 1)
            dve.wait_ge(counted, 1)
            half = LEVELS // 2
            for b in range(2):
                sl = slice(b * half, (b + 1) * half)
                do(V.tensor_copy(total[:, sl, :], ps_tot[b][:, 0:half * T].rearrange("p (l t) -> p l t", t=T)))
                do(V.tensor_copy(pre[0][:, sl, PAD:], ps_tot[b][:, 0:half * T].rearrange("p (l t) -> p l t", t=T)))
            after()
            cur = 0
            for shift in (1, 2, 4, 8, 16):
                do(V.tensor_tensor(pre[1 - cur][:, :, PAD:], pre[cur][:, :, PAD:], pre[cur][:, :, PAD - shift:PAD - shift + T], ALU.add)); after()
                cur = 1 - cur
            tiles_incl = pre[cur]
            do(V.tensor_copy(lev[0][:, PAD:], tiles_incl[:, :, PAD + T - 1])); after()
            cur = 0
            for shift in (1, 2, 4, 8, 16):
                do(V.tensor_tensor(lev[1 - cur][:, PAD:], lev[cur][:, PAD:], lev[cur][:, PAD - shift:PAD - shift + LEVELS], ALU.add)); after()
                cur = 1 - cur
            levels_incl = lev[cur]
            dve.wait_ge(pool_made, 12 + LEVELS - 1)
            do(V.tensor_tensor(over[:, 0:LEVELS - 1], levels_incl[:, PAD:PAD + LEVELS - 1], caps[:, :], ALU.is_gt))
            do(V.tensor_single_scalar(over[:, LEVELS - 1:LEVELS], levels_incl[:, PAD + LEVELS - 2:PAD + LEVELS - 1], float(N - P), op=ALU.is_lt))
            after()
            do(V.tensor_reduce(flag_f[:, :], over[:, :], AX.X, ALU.add)); after()
            do(V.tensor_copy(flag_i[:, :], flag_f[:, :])); after()
            do(V.tensor_tensor(place[:, :, :], tiles_incl[:, :, PAD:], total[:, :, :], ALU.subtract))
            do(V.tensor_tensor(lev[1 - cur][:, PAD:], levels_incl[:, PAD:], tiles_incl[:, :, PAD + T - 1], ALU.subtract)); after()
            do(V.tensor_tensor(place[:, :, :], place[:, :, :], lev[1 - cur][:, PAD:].unsqueeze(2).to_broadcast([P, LEVELS, T]), ALU.add)); after()
            for b in range(2):
                sl = slice(b * half, (b + 1) * half)
                do(V.tensor_tensor(place[:, sl, :], place[:, sl, :], ps_lt[b][:, 0:half * T].rearrange("p (l t) -> p l t", t=T), ALU.add))
            after()
            do(V.tensor_tensor(total[:, :, :], place[:, :, :], onehot[:, :, :], ALU.mult)); after()
            do(V.tensor_reduce(small[:, 3, :], total[:, :, :].rearrange("p l t -> p t l"), AX.X, ALU.add)); after()
            V.tensor_copy(rank_i[:, :], small[:, 3, :]).then_inc(ranks_made, 1)
            V.tensor_scalar_add(record[:, :, C_RANK], small[:, 3, :], 1.0).then_inc(ranks_made, 1)
            dve.wait_ge(score_copied, T // 4)
            V.tensor_reduce(best_dst[:, 0:1], record[:, :, C_SDST], AX.X, ALU.max).then_inc(tops_made, 1)
            V.engine_nop().then_inc(flag_made, 1)
            big_degree = dve.value_load(flag_i[0:1, 0:1], min_val=0, max_val=64)
            with dve.If(big_degree == 0):
                LAST = T - 1

                def bc(ap, shape, axis):
                    return ap.unsqueeze(axis).to_broadcast(shape)

                dve.wait_ge(lists_loaded, 16)
                dve.wait_ge(best_made, 1)
                V.tensor_scalar(diag[:, :], ident[:, :], ranked[:, LAST, C_SSRC:C_SSRC + 1], None, ALU.mult).then_inc(diag_made, 1)
                do(V.tensor_single_scalar(has_nbr[:, :], ranked[:, :, C_DEG], 0.0, op=ALU.is_gt)); after()
                do(V.tensor_scalar(no_nbr[:, :], has_nbr[:, :], -1.0, 1.0, ALU.mult, ALU.add))
                dve.wait_ge(src_spread, 1)
                src_row = ps_small[:, 128:256]
                do(V.tensor_scalar_add(row_max[:, 0, :], src_row, best_dst[:, 1:2])); after()
                do(V.scalar_tensor_tensor(row_max[:, 1, :], row_max[:, 0, :], SLOPE, row_max[:, 0, :], ALU.mult, ALU.max)); after()
                do(V.tensor_scalar_add(row_max[:, 0, :], row_max[:, 1, :], MASKED)); after()
                flat = big[:, 0, 0:T * F]
                do(V.tensor_tensor(weights_t, bc(src_row, [P, T, P], 1), bc(record[:, :, C_SDST], [P, T, P], 2), ALU.add)); after()
                do(V.scalar_tensor_tensor(flat, flat, SLOPE, flat, ALU.mult, ALU.max)); after()
                do(V.tensor_scalar_add(flat, flat, MASKED)); after()
                V.tensor_tensor(weights_t, weights_t, bc(row_max[:, 0, :], [P, T, P], 1), ALU.subtract).then_inc(lone_scored, 1)

                norms = 0

                def y_free(layer, g):
                    if g:
                        dve.wait_ge(layer_done[layer], g)
                    elif layer:
                        dve.wait_ge(layer_done[layer - 1], len(GROUPS))

                def norm(layer, t0, n):
                    nonlocal norms
                    for i in range(n):
                        do(V.bn_stats(moments[:, i, :], y[:, i, :]))
                    after()
                    for i in range(n):
                        do(V.bn_aggr(mean_var[:, i, :], moments[:, i, :]))
                    after()
                    V.tensor_scalar_add(stat[:, 5, 0:n], mean_var[:, 0:n, 1], EPS).then_inc(variance_ready, 1)
                    norms += 1
                    dve.wait_ge(deviation_ready, norms)
                    do(V.reciprocal(stat[:, 7, 0:n], stat[:, 6, 0:n])); after()
                    for i in range(n):
                        last = V.tensor_scalar(ranked[:, t0 + i, 0:F], y[:, i, :], mean_var[:, i, 0:1], stat[:, 7, i:i + 1],
                                               ALU.subtract, ALU.mult)
                    last.then_inc(layer_done[layer], 1)

                def attention(layer, width, s_src, first):
                    def scores(g):
                        t0, n, depth, s0 = GROUPS[g]
                        dve.wait_ge(gathered[g], 16 * n * depth * (layer + 1))
                        rows = gat(width, s0, n * depth).rearrange("p (t k f) -> p t k f", t=n, k=depth)
                        z = score[:, g % 2, 0:n * depth]
                        z3 = z.rearrange("p (t k) -> p t k", t=n)
                        do(V.tensor_tensor(z3, rows[:, :, :, C_SDST], bc(s_src[:, t0:t0 + n], [P, n, depth], 2), ALU.add)); after()
                        if layer == 0:
                            do(V.tensor_copy(nbr_rank[:, s0:s0 + n * depth].rearrange("p (t k) -> p t k", t=n), rows[:, :, :, C_RANK]))
                        do(V.scalar_tensor_tensor(z, z, SLOPE, z, ALU.mult, ALU.max)); after()
                        do(V.tensor_reduce(stat[:, g % 2, 0:n], z3, AX.X, ALU.max)); after()
                        V.tensor_tensor(z3, z3, bc(stat[:, g % 2, 0:n], [P, n, depth], 2), ALU.subtract).then_inc(scores_ready, 1)

                    def weigh(g):
                        t0, n, depth, s0 = GROUPS[g]
                        dve.wait_ge(exps_ready, first + g + 1)
                        rows = gat(width, s0, n * depth).rearrange("p (s f) -> p s f", f=width)[:, :, 0:F]
                        p2 = score[:, g % 2, 0:n * depth]
                        do(V.tensor_reduce(stat[:, 2, 0:n], p2.rearrange("p (t k) -> p t k", t=n), AX.X, ALU.add)); after()
                        do(V.reciprocal(stat[:, 3, 0:n], stat[:, 2, 0:n]))
                        do(V.tensor_tensor(rows, rows, bc(p2, [P, n * depth, F], 2), ALU.mult)); after()
                        agg = y[:, 0:n, :]
                        y_free(layer, g)
                        if depth > 1:
                            do(V.tensor_reduce(agg, rows.rearrange("p (t k) f -> p t f k", k=depth), AX.X, ALU.add)); after()
                            src = agg
                        else:
                            src = rows
                        for i in range(n):
                            do(V.scalar_tensor_tensor(y[:, i, :], src[:, i, :], stat[:, 3, i:i + 1], ranked[:, t0 + i, 0:F], ALU.mult, ALU.add))
                        after()
                        if t0 + n == T:
                            i = n - 1
                            do(V.scalar_tensor_tensor(y[:, i, :], (lone if layer == 0 else h_mean)[:, :], no_nbr[:, LAST:T],
                                                      y[:, i, :], ALU.mult, ALU.add)); after()
                        norm(layer, t0, n)

                    scores(0)
                    for g in range(len(GROUPS)):
                        if g + 1 < len(GROUPS):
                            scores(g + 1)
                        if g + 1 == len(GROUPS) and layer == 0:
                            dve.wait_ge(lone_summed, 1)
                            do(V.reciprocal(lone_sum[:, :], ps_small[:, 256:257])); after()
                            do(V.tensor_scalar(lone[:, :], ps_acc[:, 0:F], lone_sum[:, :], None, ALU.mult)); after()
                        weigh(g)

                def neighbour_max(layer):
                    for g, (t0, n, depth, s0) in enumerate(GROUPS):
                        dve.wait_ge(gathered[g], 16 * n * depth * (layer + 1))
                        rows = gat(F, s0, n * depth).rearrange("p (t k f) -> p t f k", t=n, k=depth)
                        own = ranked[:, t0:t0 + n, 0:F]
                        y_free(layer, g)
                        if depth > 1:
                            do(V.tensor_reduce(y[:, 0:n, :], rows, AX.X, ALU.max)); after()
                            do(V.tensor_tensor(y[:, 0:n, :], y[:, 0:n, :], own, ALU.add)); after()
                        else:
                            for i in range(n):
                                do(V.scalar_tensor_tensor(y[:, i, :], rows[:, i, :, 0], has_nbr[:, t0 + i:t0 + i + 1],
                                                          ranked[:, t0 + i, 0:F], ALU.mult, ALU.add))
                            after()
                        norm(layer, t0, n)

                dve.wait_ge(x_ranked, 16)
                attention(0, W0, ranked[:, :, C_SSRC], 0)
                neighbour_max(1)
                neighbour_max(2)
                dve.wait_ge(mean_made, 1)
                do(V.tensor_copy(h_mean[:, :], ps_acc[:, 128:128 + F])); after()
                attention(3, W3, h[:, :, F + 1], len(GROUPS))
            with dve.Else():
                for layer in range(4):
                    d = DENSE[layer]

                    turn_steps = 0

                    def did(ins):
                        nonlocal turn_steps
                        turn_steps += 1
                        ins.then_inc(d["step"], 1)

                    def turned(t):
                        dve.wait_ge(d["step"], t * STEPS[layer] + turn_steps)

                    def finish(t, agg, scale):
                        did(V.tensor_copy(d_own[:, :], record[:, bass.ds(t, 1), 0:F].rearrange("p a f -> p (a f)"))); turned(t)
                        if scale is None:
                            did(V.tensor_tensor(d_y[:, 0, :], agg, d_own[:, :], ALU.add)); turned(t)
                        else:
                            did(V.scalar_tensor_tensor(d_y[:, 0, :], agg, scale, d_own[:, :], ALU.mult, ALU.add)); turned(t)
                        did(V.bn_stats(d_mom[:, :], d_y[:, 0, :])); turned(t)
                        did(V.tensor_copy(d_col[:, 6:7], d_mom[:, 0:1]))
                        did(V.bn_aggr(d_mv[:, :], d_mom[:, :])); turned(t)
                        V.tensor_scalar_add(d_col[:, 3:4], d_mv[:, 1:2], EPS).then_inc(d["var"], 1)
                        dve.wait_ge(d["dev"], t + 1)
                        did(V.reciprocal(d_col[:, 5:6], d_col[:, 4:5])); turned(t)
                        did(V.tensor_scalar(d_y[:, 1, :], d_y[:, 0, :], d_mv[:, 0:1], d_col[:, 5:6], ALU.subtract, ALU.mult)); turned(t)
                        assert turn_steps == STEPS[layer], (layer, turn_steps)

                    if layer:
                        dve.wait_ge(d["x_in"], 16)
                    if layer in (0, 3):
                        if layer == 0:
                            V.tensor_copy(ranked[:, :, 0:W0], record[:, :, 0:W0]).then_inc(d["v_ready"], 1)
                        dve.wait_ge(d["v_ready"], 1 if layer == 0 else T)
                        dve.wait_ge(d["dst_in"], 16)
                        with dve.Fori(0, T) as t:
                            turn_steps = 0
                            did(V.tensor_copy(d_col[:, 0:1], ranked[:, bass.ds(t, 1), C_SSRC])); turned(t)
                            did(V.tensor_scalar(d_e, d_dst, d_col[:, 0:1], None, ALU.add)); turned(t)
                            did(V.scalar_tensor_tensor(d_e, d_e, SLOPE, d_e, ALU.mult, ALU.max))
                            dve.wait_ge(d["adj"], t * 16 + 16)
                            did(V.tensor_single_scalar(d_m, d_adj[0], 0.0, op=ALU.is_gt)); turned(t)
                            low = -MASKED if layer == 0 else 9e15
                            if layer == 3:
                                did(V.tensor_tensor(d_e, d_e, d_m, ALU.mult)); turned(t)
                            did(V.tensor_scalar(d_m, d_m, low, -low, ALU.mult, ALU.add)); turned(t)
                            did(V.tensor_tensor(d_e, d_e, d_m, ALU.add)); turned(t)
                            did(V.tensor_reduce(d_col[:, 1:2], d_e, AX.X, ALU.max, negate=True)); turned(t)
                            V.tensor_copy(d_col[:, 7:8], d_col[:, 1:2]).then_inc(d["score"], 1)
                            dve.wait_ge(d["exp"], t + 1)
                            did(V.reciprocal(d_col[:, 7:8], d_col[:, 2:3])); turned(t)
                            dve.wait_ge(d["acc"], t + 1)
                            finish(t, ps_acc[:, 0:F], d_col[:, 7:8])
                            dve.wait_ge(d["stored"], t * 16 + 16)
                    else:
                        dve.wait_ge(d["x_copied"], T // 4)
                        rows = (d["row_even"], d["row_odd"])
                        with dve.Fori(0, N // 2) as pair:
                            for b in range(2):
                                dve.wait_ge(rows[b], pair * 16 + 16)
                                V.tensor_scalar(d_e, d_adj[b], 0.0, LOWEST, ALU.is_equal, ALU.mult).then_inc(d["row_read"], 1)
                                dve.wait_ge(d["row_read"], pair * 2 + (b + 1))
                                V.tensor_reduce(d_has[:, bass.ds(pair * 2 + b, 1)], d_e, AX.X, ALU.max).then_inc(d["row_step"], 1)
                                V.tensor_tensor(d_m, d_e, d_xt, ALU.add).then_inc(d["row_step"], 1)
                                dve.wait_ge(d["row_step"], pair * 6 + (3 * b + 2))
                                V.tensor_reduce(d_max_t[:, bass.ds(pair * 2 + b, 1)], d_m, AX.X, ALU.max).then_inc(d["row_step"], 1)
                                dve.wait_ge(d["row_step"], pair * 6 + (3 * b + 3))
                        V.tensor_single_scalar(d_m, d_has, 0.0, op=ALU.is_equal).then_inc(d["row_read"], 1)
                        dve.wait_ge(d["row_read"], N + 1)
                        V.tensor_tensor(d_max_t, d_max_t, d_m, ALU.mult).then_inc(d["maxed"], 1)
                        with dve.Fori(0, T) as t:
                            turn_steps = 0
                            dve.wait_ge(d["back"], t + 1)
                            finish(t, ps_mm[0][:, 0:P], None)
                            dve.wait_ge(d["stored"], t * 16 + 16)


_INS = ["x", "adj", "L0_gnn_attn", "L3_gnn_W", "L3_gnn_a"]


def kernel(**inputs):
    import numpy as _np
    import concourse.bacc as _bacc
    from concourse import mybir as _mybir
    from concourse.bass_utils import run_bass_kernel_spmd as _run

    nc = _bacc.Bacc("TRN2", target_bir_lowering=False, num_devices=1)
    arrays, args = {}, []
    for name in _INS:
        a = _np.ascontiguousarray(inputs[name])
        arrays[f"in_{name}_dram"] = a
        args.append(nc.dram_tensor(f"in_{name}_dram", a.shape, _mybir.dt.from_np(a.dtype), kind="ExternalInput").ap())
    args.append(nc.dram_tensor("out_0_dram", (4096, 128), _mybir.dt.float32, kind="ExternalOutput").ap())
    gnn_kernel(nc, *args)
    r = _run(nc, [arrays], core_ids=[0])
    return r.results[0]["out_0_dram"]
```

```python
from contextlib import ExitStack

import concourse.bass as bass
from concourse import mybir

ALU = mybir.AluOpType
ACT = mybir.ActivationFunctionType
AX = mybir.AxisListType
F32 = mybir.dt.float32
BF16 = mybir.dt.bfloat16
I32 = mybir.dt.int32
U32 = mybir.dt.uint32
U16 = mybir.dt.uint16

P = 128
F = 128
N = 4096
T = N // P
SLOTS = 16
FOLDS = 4
FOLDED = N // FOLDS
SEARCHES = 8
KEY_SHIFT = 14
QUAD = 4
QUADS = T // QUAD
EPS = 1e-5
SLOPE = 0.2
MASKED = -1e9
LOWEST = -3.4028234663852886e38
FAR = -1e30

SERVED = [32, 30, 26, 20, 13, 8, 5, 3] + [1] * 8
DEPTH = [sum(n > t for n in SERVED) for t in range(T)]
GATHERS = sum(DEPTH)
_RUNS = [(26, 4), (20, 6), (0, 1), (13, 4), (1, 2), (8, 3), (30, 2), (11, 2), (5, 3), (3, 2), (17, 2), (19, 1)]
GROUPS = []
for _t, _n in _RUNS:
    assert len({DEPTH[_t + _i] for _i in range(_n)}) == 1
    GROUPS.append((_t, _n, DEPTH[_t], sum(n * k for _, n, k, _ in GROUPS)))
assert sorted(t + i for t, n, _, _ in GROUPS for i in range(n)) == list(range(T))
BATCH = 3
LEVELS = SLOTS + 2

STEPS = {0: 15, 1: 7, 2: 7, 3: 16}

C_SDST, C_RANK, C_SSRC, C_DEG, C_NBR, C_ID = F, F + 1, F + 2, F + 3, F + 4, F + 4 + SLOTS
RECORD = C_ID + 1
W0 = F + 4
W3 = F + 2


def gnn_kernel(nc, x, adj, attn, w, a3, out):
    with ExitStack() as ctx:
        def sb(name, shape, dt):
            return ctx.enter_context(nc.sbuf_tensor(name, shape, dt))

        def ps(name, shape, dt=F32):
            return ctx.enter_context(nc.psum_tensor(name, shape, dt))

        def sem(name):
            return ctx.enter_context(nc.semaphore(name))

        table0 = nc.dram_tensor("table0", [N + 1, W0], F32).ap()
        table1 = nc.dram_tensor("table1", [N + 1, F], F32).ap()
        table2 = nc.dram_tensor("table2", [N + 1, F], F32).ap()
        table3 = nc.dram_tensor("table3", [N + 1, W3], F32).ap()
        ranked_dram = nc.dram_tensor("ranked_dram", [N, RECORD], F32).ap()
        dense_dram = [nc.dram_tensor(f"dense_dram{i}", [N, F], F32).ap() for i in range(3)]
        dst_dram = {i: nc.dram_tensor(f"dst_dram{i}", [N], F32).ap() for i in (0, 3)}

        work = sb("work", [P, GATHERS * W0], F32)
        adj_buf = [work[:, b * N:(b + 1) * N].bitcast(I32) for b in range(QUAD)]
        column_w = sb("column_w", [P, FOLDED], F32)
        fold_w = sb("fold_w", [P, FOLDS, P], BF16)
        record = sb("record", [P, T, RECORD], F32)
        record_i = record[:, :, :].bitcast(I32)
        ranked = sb("ranked", [P, T, RECORD], F32)
        ranked_i = ranked[:, :, :].bitcast(I32)
        big = sb("big", [P, 2, T * (F + 4)], F32)
        mask_buf = [big[:, b // 2, (b % 2) * (N // 2):(b % 2 + 1) * (N // 2)].bitcast(BF16) for b in range(QUAD)]
        key_buf = [ranked[:, :, :].rearrange("p t r -> p (t r)")[:, b * FOLDED:(b + 1) * FOLDED] for b in range(QUAD)]
        weights_t = big[:, 0, 0:T * F].rearrange("p (t i) -> p t i", t=T)
        h = big[:, 1, 0:T * W3].rearrange("p (t f) -> p t f", t=T)
        ident = sb("ident", [P, P], F32)
        ones = sb("ones", [P, P], F32)
        attn_cols = sb("attn_cols", [P, 2], F32)
        a3_cols = sb("a3_cols", [P, 2], F32)
        w_aug = sb("w_aug", [P, W3], F32)
        w_t = sb("w_t", [P, F], F32)
        x_t = sb("x_t", [P, 2, 4 * P], F32)
        empty = sb("empty", [1, 4, W0], F32)
        found = sb("found", [P, 2, QUAD, 64], F32)
        top16 = sb("top16", [P, QUAD, SLOTS], F32)
        edge = sb("edge", [P, QUAD, FOLDS, SLOTS], F32)
        edge_left = sb("edge_left", [P, QUAD, FOLDS * SLOTS], F32)
        key_i = sb("key_i", [P, 4, QUAD, SLOTS], I32)
        key_f = sb("key_f", [P, 3, QUAD, SLOTS], F32)
        bits = sb("bits", [P, FOLDS, QUAD, SLOTS], I32)
        held_word = sb("held_word", [P, 16], F32)
        row_sum = sb("row_sum", [P, T], F32)
        low_bf = sb("low_bf", [P, P], BF16)
        ones_bf = sb("ones_bf", [P, P], BF16)
        held = sb("held", [P, T, SLOTS], F32)
        small = sb("small", [P, 4, T], F32)
        level_of = sb("level_of", [P, LEVELS, T], F32)
        onehot = sb("onehot", [P, LEVELS, T], BF16)
        PAD = 16
        pre = [sb(f"pre{b}", [P, LEVELS, PAD + T], F32) for b in range(2)]
        lev = [sb(f"lev{b}", [P, PAD + LEVELS], F32) for b in range(2)]
        place = sb("place", [P, LEVELS, T], F32)
        total = sb("total", [P, LEVELS, T], F32)
        rank_i = sb("rank_i", [P, T], I32)
        caps = sb("caps", [P, LEVELS - 1], F32)
        over = sb("over", [P, LEVELS], F32)
        flag_f = sb("flag_f", [P, 1], F32)
        flag_i = sb("flag_i", [P, 1], I32)
        nbr_rank = sb("nbr_rank", [P, GATHERS], I32)
        maxn = max(n for _, n, _, _ in GROUPS)
        maxs = max(n * k for _, n, k, _ in GROUPS)
        score = sb("score", [P, 2, maxs], F32)
        stat = sb("stat", [P, 8, maxn], F32)
        y = sb("y", [P, 2, maxn, F], F32)
        norm_scale = sb("norm_scale", [P, 2, maxn], F32)
        norm_shift = sb("norm_shift", [P, 2, maxn], F32)
        moments = sb("moments", [P, maxn, 6], F32)
        mean_var = sb("mean_var", [P, maxn, 2], F32)
        has_nbr = sb("has_nbr", [P, T], F32)
        no_nbr = sb("no_nbr", [P, T], F32)
        best_dst = sb("best_dst", [P, 2], F32)
        diag = sb("diag", [P, P], F32)
        row_max = sb("row_max", [P, 2, P], F32)
        lone = sb("lone", [P, F], F32)
        lone_sum = sb("lone_sum", [P, 1], F32)
        h_mean = sb("h_mean", [P, F], F32)
        x3_t = sb("x3_t", [P, 2, BATCH * P], F32)
        mean_w = sb("mean_w", [P, P], F32)

        d_adj = [work[:, b * N:(b + 1) * N].bitcast(I32) for b in range(2)]
        d_e = work[:, 2 * N:3 * N]
        d_m = work[:, 3 * N:4 * N]
        d_dst = big[:, 0, 0:N]
        d_xt = big[:, 0, 0:N]
        d_pt = big[:, 1, 0:N]
        d_max_t = big[:, 1, 0:N]
        d_has = ranked[:, :, :].rearrange("p t r -> p (t r)")[:, 0:N]
        d_y = sb("d_y", [P, 2, F], F32)
        d_own = sb("d_own", [P, F], F32)
        d_col = sb("d_col", [P, 8], F32)
        d_mom = sb("d_mom", [P, 6], F32)
        d_mv = sb("d_mv", [P, 2], F32)

        ps_fold = [ps(f"ps_fold{b}", [P, FOLDED]) for b in range(2)]
        ps_tr = [ps_fold[0][:, b * 512:(b + 1) * 512] for b in range(2)]
        ps_mm = [ps_fold[1][:, b * 512:(b + 1) * 512] for b in range(2)]
        ps_small = ps("ps_small", [P, 512])
        ps_acc = ps("ps_acc", [P, 512])
        ps_x = [ps(f"ps_x{b}", [P, 4 * P]) for b in range(2)]
        ps_lt = [ps_tr[0], ps_tr[1]]
        ps_tot = [ps_mm[0], ps_mm[1]]

        adj_loaded = [sem(f"adj_loaded{b}") for b in range(QUAD)]
        masked = sem("masked")
        folded = sem("folded")
        keyed = sem("keyed")
        searched = sem("searched")
        attn_loaded = sem("attn_loaded")
        w_loaded = sem("w_loaded")
        x_loaded = sem("x_loaded")
        pool_made = sem("pool_made")
        x_transposed = sem("x_transposed")
        xt_copied = sem("xt_copied")
        scored = sem("scored")
        score_copied = sem("score_copied")
        w_turned = sem("w_turned")
        wt_copied = sem("wt_copied")
        wa_made = sem("wa_made")
        wa_copied = sem("wa_copied")
        dve_step = sem("dve_step")
        onehot_made = sem("onehot_made")
        counted = sem("counted")
        ranks_made = sem("ranks_made")
        flag_made = sem("flag_made")
        tops_made = sem("tops_made")
        best_made = sem("best_made")
        empty_written = sem("empty_written")
        table0_written = sem("table0_written")
        scattered = sem("scattered")
        lists_loaded = sem("lists_loaded")
        x_ranked = sem("x_ranked")
        gathered = [sem(f"gathered{g}") for g in range(len(GROUPS))]
        scores_ready = sem("scores_ready")
        exps_ready = sem("exps_ready")
        variance_ready = sem("variance_ready")
        shift_ready = sem("shift_ready")
        deviation_ready = sem("deviation_ready")
        diag_made = sem("diag_made")
        src_spread = sem("src_spread")
        lone_scored = sem("lone_scored")
        lone_exp = sem("lone_exp")
        lone_summed = sem("lone_summed")
        layer_done = [sem(f"layer{i}_done") for i in range(4)]
        table_written = {i: sem(f"table{i}_written") for i in (1, 2, 3)}
        x3_turned = sem("x3_turned")
        x3t_copied = sem("x3t_copied")
        h_made = sem("h_made")
        h_copied = sem("h_copied")
        mean_made = sem("mean_made")
        out_written = sem("out_written")
        DENSE = {}
        for layer in range(4):
            names = ["x_in", "step", "dev", "var", "stored"]
            if layer in (0, 3):
                names += ["v_ready", "dst_out", "dst_in", "adj", "score", "exp", "turned", "copied", "acc"]
            if layer == 3:
                names += ["x_turned", "x_copied", "h_made"]
            if layer in (1, 2):
                names += ["x_turned", "x_copied", "row_even", "row_odd", "row_read", "row_step", "maxed", "back"]
            DENSE[layer] = {k: sem(f"dense{layer}_{k}") for k in names}

        block = ctx.enter_context(nc.Block())

        POOL_MADE = 12 + (LEVELS - 1) + 2 * FOLDS

        batches, made_so_far = [], 0
        for t0, n, _, _ in GROUPS:
            starts = range(0, n, BATCH)
            batches.append([(made_so_far + j, t0 + i, min(BATCH, n - i)) for j, i in enumerate(starts)])
            made_so_far += len(starts)

        X_STEPS = [range(0, 0), range(0, 3), range(3, 6), range(6, T // 4)]

        def gat(width, slot, count):
            return work[:, slot * width:(slot + count) * width]

        @block.sync
        def _(sp):
            for b in range(QUAD):
                sp.dma_start(adj_buf[b], adj[b * P:(b + 1) * P, :]).then_inc(adj_loaded[b], 16)
                if b == 0:
                    sp.dma_start(record[:, :, 0:F], x.rearrange("(t p) f -> p t f", p=P)).then_inc(x_loaded, 16)
            with sp.Fori(0, QUADS - 1) as quad:
                for b in range(QUAD):
                    sp.wait_ge(masked, quad * QUAD + (b + 1))
                    sp.dma_start(adj_buf[b], adj[bass.ds(quad * (QUAD * P) + (QUAD + b) * P, P), :]).then_inc(adj_loaded[b], 16)
            sp.wait_ge(ranks_made, 2)
            sp.wait_ge(score_copied, 1)
            sp.wait_ge(x_loaded, 16)
            sp.dma_start(table0[1:N + 1, :].rearrange("(t p) f -> p t f", p=P),
                         record[:, :, 0:W0]).then_inc(table0_written, 16)
            sp.wait_ge(flag_made, 1)
            big_degree = sp.value_load(flag_i[0:1, 0:1], min_val=0, max_val=64)
            with sp.If(big_degree == 0):
                sp.wait_ge(scattered, 16 * T)
                sp.dma_start(ranked[:, :, C_SDST:RECORD],
                             ranked_dram.rearrange("(t p) f -> p t f", p=P)[:, :, C_SDST:RECORD]).then_inc(lists_loaded, 16)
                for layer, table, width in ((1, table1, F), (2, table2, F)):
                    for g, (t0, n, _, _) in enumerate(GROUPS):
                        sp.wait_ge(layer_done[layer - 1], g + 1)
                        sp.dma_start(table[1 + t0 * P:1 + (t0 + n) * P, :].rearrange("(t p) f -> p t f", p=P),
                                     ranked[:, t0:t0 + n, 0:F]).then_inc(table_written[layer], 16)
                for g, (t0, n, _, _) in enumerate(GROUPS):
                    sp.wait_ge(h_copied, batches[g][-1][0] + 1)
                    sp.dma_start(table3[1 + t0 * P:1 + (t0 + n) * P, :].rearrange("(t p) f -> p t f", p=P),
                                 h[:, t0:t0 + n, :]).then_inc(table_written[3], 16)
            with sp.Else():
                for layer in range(4):
                    d = DENSE[layer]
                    to = out if layer == 3 else dense_dram[layer]
                    if layer:
                        sp.wait_ge(table0_written, 16)
                        sp.wait_ge(DENSE[layer - 1]["stored"], 16 * T)
                        sp.dma_start(record[:, :, 0:F], dense_dram[layer - 1].rearrange("(t p) f -> p t f", p=P)).then_inc(d["x_in"], 16)
                    if layer in (0, 3):
                        sp.wait_ge(d["v_ready"], 1 if layer == 0 else T)
                        sp.dma_start(dst_dram[layer].rearrange("(t p) -> p t", p=P), ranked[:, :, C_SDST],
                                     allow_slow_non_contiguous=True).then_inc(d["dst_out"], 16)
                        sp.wait_ge(d["dst_out"], 16)
                        sp.dma_start(d_dst, dst_dram[layer].partition_broadcast(P)).then_inc(d["dst_in"], 16)
                        with sp.Fori(0, T) as t:
                            sp.dma_start(d_adj[0], adj[bass.ds(t * P, P), :]).then_inc(d["adj"], 16)
                            sp.wait_ge(d["step"], t * STEPS[layer] + STEPS[layer])
                            sp.dma_start(to[bass.ds(t * P, P), :], d_y[:, 1, :]).then_inc(d["stored"], 16)
                    else:
                        rows = (d["row_even"], d["row_odd"])
                        for b in range(2):
                            sp.dma_start(d_adj[b], adj[b, :].partition_broadcast(P)).then_inc(rows[b], 16)
                        with sp.Fori(0, N // 2 - 1) as pair:
                            for b in range(2):
                                sp.wait_ge(d["row_read"], pair * 2 + (b + 1))
                                sp.dma_start(d_adj[b], adj[bass.ds(pair * 2 + (2 + b), 1), :].rearrange("a n -> (a n)").partition_broadcast(P)).then_inc(rows[b], 16)
                        with sp.Fori(0, T) as t:
                            sp.wait_ge(d["step"], t * STEPS[layer] + STEPS[layer])
                            sp.dma_start(to[bass.ds(t * P, P), :], d_y[:, 1, :]).then_inc(d["stored"], 16)
                sp.wait_ge(DENSE[3]["stored"], 16 * T)

        @block.gpsimd
        def _(pool):
            made = 0

            def make(ins):
                nonlocal made
                made += 1
                ins.then_inc(pool_made, 1)
                return made

            make(nc.gpsimd.iota(column_w[:, :], pattern=[[1, FOLDED]], base=1 << KEY_SHIFT, channel_multiplier=0,
                                allow_small_or_imprecise_dtypes=True))
            make(nc.gpsimd.memset(ones[:, :], 1.0))
            pool.wait_ge(pool_made, made)
            make(nc.gpsimd.affine_select(out=ident[:, :], in_=ones[:, :], pattern=[[1, P]],
                                         compare_op=ALU.is_equal, fill=0.0, base=0, channel_multiplier=-1))
            make(nc.gpsimd.memset(ones_bf[:, :], 1.0))
            pool.wait_ge(pool_made, made)
            make(nc.gpsimd.affine_select(out=low_bf[:, :], in_=ones_bf[:, :], pattern=[[1, P]],
                                         compare_op=ALU.is_gt, fill=0.0, base=0, channel_multiplier=-1))
            make(nc.gpsimd.iota(level_of[:, :, :], pattern=[[-1, LEVELS], [0, T]], base=LEVELS - 1,
                                channel_multiplier=0, allow_small_or_imprecise_dtypes=True))
            make(nc.gpsimd.iota(record_i[:, :, C_ID], pattern=[[P, T]], base=0, channel_multiplier=1))
            make(nc.gpsimd.memset(mean_w[:, :], 1.0 / N))
            make(nc.gpsimd.memset(empty[:, :, :], 0.0))
            pool.wait_ge(pool_made, made)
            make(nc.gpsimd.memset(empty[:, 0, C_SDST:C_SDST + 1], FAR))
            make(nc.gpsimd.memset(empty[:, 1, :], LOWEST))
            make(nc.gpsimd.memset(empty[:, 3, C_SDST:C_SDST + 1], FAR))
            make(nc.gpsimd.memset(caps[:, 0:1], 0.0))
            for level in range(1, LEVELS - 1):
                make(nc.gpsimd.memset(caps[:, level:level + 1], float(P * SERVED[SLOTS - level])))
            for k in range(FOLDS):
                make(nc.gpsimd.memset(fold_w[:, k, :], float(1 << k)))
            pool.wait_ge(pool_made, made)
            for k in range(FOLDS):
                make(nc.gpsimd.affine_select(out=fold_w[:, k, :], in_=fold_w[:, k, :], pattern=[[1, P]],
                                             compare_op=ALU.is_equal, fill=0.0, base=0, channel_multiplier=-1))
            assert made == POOL_MADE
            pool.wait_ge(tops_made, 1)
            nc.gpsimd.partition_all_reduce(best_dst[:, 1:2], best_dst[:, 0:1], P,
                                           bass.bass_isa.ReduceOp.max).then_inc(best_made, 1)
            pool.wait_ge(flag_made, 1)
            big_degree = pool.value_load(flag_i[0:1, 0:1], min_val=0, max_val=64)
            with pool.If(big_degree == 0):
                pool.wait_ge(ranks_made, 2)
                pool.wait_ge(score_copied, 1)
                pool.wait_ge(x_loaded, 16)
                for t in range(T):
                    pool.indirect_dma_start(out=ranked_dram, out_offset=bass.IndirectOffsetOnAxis(ap=rank_i[:, t:t + 1], axis=0),
                                            in_=record[:, t, :], in_offset=None).then_inc(scattered, 16)
                pool.wait_ge(lists_loaded, 16)
                pool.wait_ge(table0_written, 16)
                pool.wait_ge(empty_written, 16 * 4)

                def gather(table, width, index):
                    for g, (t0, n, depth, s0) in enumerate(GROUPS):
                        for t in range(t0, t0 + n):
                            for k in range(depth):
                                s = s0 + (t - t0) * depth + k
                                pool.indirect_dma_start(
                                    out=gat(width, s, 1), out_offset=None, in_=table,
                                    in_offset=bass.IndirectOffsetOnAxis(ap=index(t, s, k), axis=0),
                                ).then_inc(gathered[g], 16)

                gather(table0, W0, lambda t, s, k: ranked_i[:, t, C_NBR + k:C_NBR + k + 1])
                for layer, table, width in ((1, table1, F), (2, table2, F), (3, table3, W3)):
                    pool.wait_ge(layer_done[layer - 1], len(GROUPS))
                    pool.wait_ge(table_written[layer], 16 * len(GROUPS))
                    gather(table, width, lambda t, s, k: nbr_rank[:, s:s + 1])
                for g, (t0, n, _, _) in enumerate(GROUPS):
                    pool.wait_ge(layer_done[3], g + 1)
                    for t in range(t0, t0 + n):
                        pool.indirect_dma_start(out=out, out_offset=bass.IndirectOffsetOnAxis(ap=ranked_i[:, t, C_ID:C_ID + 1], axis=0),
                                                in_=ranked[:, t, 0:F], in_offset=None).then_inc(out_written, 16)
                pool.wait_ge(out_written, 16 * T)
            with pool.Else():
                pool.wait_ge(empty_written, 16 * 4)

        @block.scalar
        def _(act):
            act.dma_start(attn_cols[:, :], attn.rearrange("(c f) o -> f (c o)", f=F), allow_slow_non_contiguous=True).then_inc(attn_loaded, 16)
            act.dma_start(a3_cols[:, :], a3.rearrange("(c f) o -> f (c o)", f=F), allow_slow_non_contiguous=True).then_inc(w_loaded, 16)
            act.dma_start(w_aug[:, 0:F], w).then_inc(w_loaded, 16)
            act.wait_ge(pool_made, 12)
            act.dma_start(table0[0:1, :], empty[:, 0, :]).then_inc(empty_written, 16)
            act.dma_start(table1[0:1, :], empty[:, 1, 0:F]).then_inc(empty_written, 16)
            act.dma_start(table2[0:1, :], empty[:, 1, 0:F]).then_inc(empty_written, 16)
            act.dma_start(table3[0:1, :], empty[:, 3, 0:W3]).then_inc(empty_written, 16)

            def x_copies(b):
                for q in X_STEPS[b]:
                    act.wait_ge(x_transposed, q + 1)
                    if q >= 2:
                        act.wait_ge(scored, q - 1)
                    nc.scalar.copy(x_t[:, q % 2, :], ps_x[q % 2][:, :]).then_inc(xt_copied, 1)
                if b == 1:
                    act.wait_ge(w_turned, 1)
                    nc.scalar.copy(w_t[:, :], ps_acc[:, 0:F]).then_inc(wt_copied, 1)
                if b == 2:
                    act.wait_ge(wa_made, 1)
                    nc.scalar.copy(w_aug[:, F:F + 1], ps_acc[:, P + 1:P + 2])
                    nc.scalar.copy(w_aug[:, F + 1:F + 2], ps_acc[:, P:P + 1]).then_inc(wa_copied, 1)

            def masks(quad, first):
                for b in range(QUAD):
                    act.wait_ge(adj_loaded[b], quad * 16 + 16)
                    if not first:
                        act.wait_ge(folded, quad * QUAD + (b + 1 - QUAD))
                    nc.scalar.activation(mask_buf[b], adj_buf[b].bitcast(U32), ACT.Copy,
                                         accum_out=row_sum[:, bass.ds(quad * QUAD + b, 1)]).then_inc(masked, 1)
                    if first:
                        x_copies(b)

            masks(0, True)
            act.wait_ge(scored, T // 4)
            scores = ps_small[:, 0:2 * T].rearrange("p (t c) -> p t c", c=2)
            nc.scalar.copy(record[:, :, C_SSRC], scores[:, :, 0])
            nc.scalar.copy(record[:, :, C_SDST], scores[:, :, 1]).then_inc(score_copied, 1)
            with act.Fori(1, QUADS) as quad:
                masks(quad, False)
            act.wait_ge(flag_made, 1)
            big_degree = act.value_load(flag_i[0:1, 0:1], min_val=0, max_val=64)
            with act.If(big_degree == 0):
                act.wait_ge(scattered, 16 * T)
                act.dma_start(ranked[:, :, 0:C_SDST],
                              ranked_dram.rearrange("(t p) f -> p t f", p=P)[:, :, 0:C_SDST]).then_inc(x_ranked, 16)

                G = len(GROUPS)

                def exponential(g, first):
                    _, n, depth, _ = GROUPS[g]
                    act.wait_ge(scores_ready, first + g + 1)
                    nc.scalar.activation(score[:, g % 2, 0:n * depth], score[:, g % 2, 0:n * depth],
                                         ACT.Exp).then_inc(exps_ready, 1)

                def root(g, layer):
                    t0, n, _, _ = GROUPS[g]
                    act.wait_ge(variance_ready, layer * G + g + 1)
                    nc.scalar.activation(stat[:, 6, 0:n], stat[:, 5, 0:n], ACT.Sqrt).then_inc(deviation_ready, 1)
                    act.wait_ge(shift_ready, layer * G + g + 1)
                    for i in range(n):
                        last = nc.scalar.activation(ranked[:, t0 + i, 0:F], y[:, g % 2, i, :], ACT.Identity,
                                                    scale=norm_scale[:, g % 2, i:i + 1], bias=norm_shift[:, g % 2, i:i + 1])
                    last.then_inc(layer_done[layer], 1)

                def attention(first, layer):
                    for g in range(G):
                        exponential(g, first)
                        root(g, layer)

                act.wait_ge(lone_scored, 1)
                nc.scalar.activation(big[:, 0, 0:T * F], big[:, 0, 0:T * F], ACT.Exp).then_inc(lone_exp, 1)
                attention(0, 0)
                for layer in (1,):
                    for g in range(G):
                        root(g, layer)
                for g in range(G + 1):
                    if g < G:
                        root(g, 2)
                    if g >= 1:
                        for j, t, n in batches[g - 1]:
                            act.wait_ge(x3_turned, j + 1)
                            nc.scalar.copy(x3_t[:, j % 2, 0:n * P], ps_tr[j % 2][:, 0:n * P]).then_inc(x3t_copied, 1)
                            act.wait_ge(h_made, j + 1)
                            nc.scalar.copy(h[:, t:t + n, :], ps_mm[j % 2][:, 0:n * W3].rearrange("p (t f) -> p t f", t=n)).then_inc(h_copied, 1)
                attention(G, 3)
            with act.Else():
                for layer in range(4):
                    d = DENSE[layer]
                    if layer == 3:
                        with act.Fori(0, T) as t:
                            act.wait_ge(d["x_turned"], t + 1)
                            nc.scalar.copy(x3_t[:, 0, 0:P], ps_tr[0][:, 0:P]).then_inc(d["x_copied"], 1)
                            act.wait_ge(d["h_made"], t + 1)
                            nc.scalar.copy(ranked[:, bass.ds(t, 1), 0:F + 1], ps_mm[0][:, 0:F + 1].unsqueeze(1))
                            nc.scalar.copy(ranked[:, bass.ds(t, 1), C_SSRC], ps_mm[0][:, F + 1:F + 2]).then_inc(d["v_ready"], 1)
                    if layer in (0, 3):
                        with act.Fori(0, T) as t:
                            act.wait_ge(d["score"], t + 1)
                            nc.scalar.activation(d_e, d_e, ACT.Exp, bias=d_col[:, 1:2], accum_out=d_col[:, 2:3]).then_inc(d["exp"], 1)
                            for q in range(T // 4):
                                act.wait_ge(d["turned"], t * (T // 4) + (q + 1))
                                nc.scalar.copy(d_pt[:, q * 4 * P:(q + 1) * 4 * P], ps_tr[q % 2][:, :]).then_inc(d["copied"], 1)
                            act.wait_ge(d["var"], t + 1)
                            nc.scalar.activation(d_col[:, 4:5], d_col[:, 3:4], ACT.Sqrt).then_inc(d["dev"], 1)
                    else:
                        for q in range(T // 4):
                            act.wait_ge(d["x_turned"], q + 1)
                            nc.scalar.copy(d_xt[:, q * 4 * P:(q + 1) * 4 * P], ps_tr[q % 2][:, :]).then_inc(d["x_copied"], 1)
                        with act.Fori(0, T) as t:
                            act.wait_ge(d["var"], t + 1)
                            nc.scalar.activation(d_col[:, 4:5], d_col[:, 3:4], ACT.Sqrt).then_inc(d["dev"], 1)

        @block.tensor
        def _(pe):
            def score(q):
                pe.wait_ge(xt_copied, q + 1)
                for j in range(4):
                    last = nc.tensor.matmul(ps_small[:, 8 * q + 2 * j:8 * q + 2 * j + 2], x_t[:, q % 2, j * P:(j + 1) * P],
                                            attn_cols[:, :], start=True, stop=True)
                last.then_inc(scored, 1)

            def x_steps(b):
                if b == 1:
                    pe.wait_ge(x_loaded, 16)
                    pe.wait_ge(attn_loaded, 16)
                for q in X_STEPS[b]:
                    if q >= 2:
                        score(q - 2)
                    for j in range(4):
                        last = nc.tensor.transpose(ps_x[q % 2][:, j * P:(j + 1) * P], record[:, 4 * q + j, 0:F], ident[:, :])
                    last.then_inc(x_transposed, 1)
                if b == 1:
                    pe.wait_ge(w_loaded, 32)
                    nc.tensor.transpose(ps_acc[:, 0:F], w_aug[:, 0:F], ident[:, :]).then_inc(w_turned, 1)
                if b == 2:
                    pe.wait_ge(wt_copied, 1)
                    nc.tensor.matmul(ps_acc[:, P:P + 2], w_t[:, :], a3_cols[:, :], start=True, stop=True).then_inc(wa_made, 1)

            pe.wait_ge(pool_made, POOL_MADE)

            def fold(quad, first):
                for b in range(QUAD):
                    if first:
                        x_steps(b)
                    pe.wait_ge(masked, quad * QUAD + (b + 1))
                    if not (first and b < 2):
                        pe.wait_ge(keyed, quad * QUAD + (b - 1))
                    for c in range(0, FOLDED, 512):
                        for k in range(FOLDS):
                            last = nc.tensor.matmul(ps_fold[b % 2][:, c:c + 512], fold_w[:, k, :],
                                                    mask_buf[b][:, k * FOLDED + c:k * FOLDED + c + 512],
                                                    start=(k == 0), stop=(k == FOLDS - 1))
                    last.then_inc(folded, 1)

            fold(0, True)
            score(T // 4 - 2)
            score(T // 4 - 1)
            with pe.Fori(1, QUADS) as quad:
                fold(quad, False)
            pe.wait_ge(onehot_made, 1)
            half = LEVELS // 2
            for b in range(2):
                ohb = onehot[:, b * half:(b + 1) * half, :].rearrange("p l t -> p (l t)")
                nc.tensor.matmul(ps_lt[b][:, 0:half * T], low_bf[:, :], ohb, start=True, stop=True)
                last = nc.tensor.matmul(ps_tot[b][:, 0:half * T], ones_bf[:, :], ohb, start=True, stop=True)
            last.then_inc(counted, 1)
            pe.wait_ge(flag_made, 1)
            big_degree = pe.value_load(flag_i[0:1, 0:1], min_val=0, max_val=64)
            with pe.If(big_degree == 0):
                pe.wait_ge(diag_made, 1)
                nc.tensor.matmul(ps_small[:, 128:256], ones[:, :], diag[:, :], start=True, stop=True).then_inc(src_spread, 1)
                pe.wait_ge(lone_exp, 1)
                for t in range(T):
                    nc.tensor.matmul(ps_acc[:, 0:F], weights_t[:, t, :], record[:, t, 0:F], start=(t == 0), stop=(t == T - 1))
                for t in range(T):
                    last = nc.tensor.matmul(ps_small[:, 256:257], weights_t[:, t, :], ones[:, 0:1], start=(t == 0), stop=(t == T - 1))
                last.then_inc(lone_summed, 1)
                def mean(j, t, n):
                    pe.wait_ge(h_copied, j + 1)
                    for i in range(n):
                        last = nc.tensor.matmul(ps_acc[:, 128:128 + F], mean_w[:, :], h[:, t + i, 0:F],
                                                start=(j == 0 and i == 0), stop=(j == batches[-1][-1][0] and i == n - 1))
                    return last

                before = None
                for g in range(len(GROUPS)):
                    pe.wait_ge(layer_done[2], g + 1)
                    for j, t, n in batches[g]:
                        for i in range(n):
                            last = nc.tensor.transpose(ps_tr[j % 2][:, i * P:(i + 1) * P], ranked[:, t + i, 0:F], ident[:, :])
                        last.then_inc(x3_turned, 1)
                        pe.wait_ge(x3t_copied, j + 1)
                        if j >= 2:
                            pe.wait_ge(h_copied, j - 1)
                        for i in range(n):
                            last = nc.tensor.matmul(ps_mm[j % 2][:, i * W3:(i + 1) * W3], x3_t[:, j % 2, i * P:(i + 1) * P], w_aug[:, :], start=True, stop=True)
                        last.then_inc(h_made, 1)
                        if before:
                            mean(*before)
                        before = j, t, n
                mean(*before).then_inc(mean_made, 1)
            with pe.Else():
                for layer in range(4):
                    d = DENSE[layer]
                    if layer:
                        pe.wait_ge(d["x_in"], 16)
                    if layer == 3:
                        for t in range(T):
                            nc.tensor.transpose(ps_tr[0][:, 0:P], record[:, t, 0:F], ident[:, :]).then_inc(d["x_turned"], 1)
                            pe.wait_ge(d["x_copied"], t + 1)
                            nc.tensor.matmul(ps_mm[0][:, 0:W3], x3_t[:, 0, 0:P], w_aug[:, :], start=True, stop=True).then_inc(d["h_made"], 1)
                            pe.wait_ge(d["v_ready"], t + 1)
                    if layer in (0, 3):
                        with pe.Fori(0, T) as t:
                            pe.wait_ge(d["exp"], t + 1)
                            for q in range(T // 4):
                                if q >= 2:
                                    pe.wait_ge(d["copied"], t * (T // 4) + (q - 1))
                                for j in range(4):
                                    c = (4 * q + j) * P
                                    last = nc.tensor.transpose(ps_tr[q % 2][:, j * P:(j + 1) * P], d_e[:, c:c + P], ident[:, :])
                                last.then_inc(d["turned"], 1)
                            pe.wait_ge(d["copied"], t * (T // 4) + T // 4)
                            for j in range(T):
                                last = nc.tensor.matmul(ps_acc[:, 0:F], d_pt[:, j * P:(j + 1) * P], ranked[:, j, 0:F], start=(j == 0), stop=(j == T - 1))
                            last.then_inc(d["acc"], 1)
                            pe.wait_ge(d["step"], t * STEPS[layer] + STEPS[layer])
                    else:
                        for q in range(T // 4):
                            if q >= 2:
                                pe.wait_ge(d["x_copied"], q - 1)
                            for j in range(4):
                                last = nc.tensor.transpose(ps_tr[q % 2][:, j * P:(j + 1) * P], record[:, 4 * q + j, 0:F], ident[:, :])
                            last.then_inc(d["x_turned"], 1)
                        pe.wait_ge(d["maxed"], 1)
                        for t in range(T):
                            nc.tensor.transpose(ps_mm[0][:, 0:P], d_max_t[:, t * P:(t + 1) * P], ident[:, :]).then_inc(d["back"], 1)
                            pe.wait_ge(d["step"], t * STEPS[layer] + STEPS[layer])

        @block.vector
        def _(dve):
            V = nc.vector
            steps = 0

            def do(ins):
                nonlocal steps
                steps += 1
                ins.then_inc(dve_step, 1)
                return steps

            def after(n=None):
                dve.wait_ge(dve_step, steps if n is None else n)

            for b in range(2):
                do(V.memset(pre[b][:, :, :], 0.0))
                do(V.memset(lev[b][:, :], 0.0))
            dve.wait_ge(pool_made, 1)
            def hold(i, ap):
                V.tensor_copy(held_word[:, i:i + 1], ap)

            QUAD_STEPS = 20
            with dve.Fori(0, QUADS) as quad:
                now = 0

                def did(ins):
                    nonlocal now
                    now += 1
                    ins.then_inc(searched, 1)

                def turned():
                    dve.wait_ge(searched, quad * QUAD_STEPS + now)

                def key(b):
                    dve.wait_ge(folded, quad * QUAD + (b + 1))
                    V.tensor_tensor(key_buf[b], ps_fold[b % 2][:, :], column_w[:, :], ALU.mult).then_inc(keyed, 1)

                def search(b):
                    dve.wait_ge(keyed, quad * QUAD + (b + 1))
                    hold(b, key_buf[b][:, 0:1])
                    part = FOLDED // SEARCHES
                    for e in range(SEARCHES):
                        last = V.max(found[:, 0, b, 8 * e:8 * e + 8], key_buf[b][:, e * part:(e + 1) * part])
                    return last

                def greatest16(out16, held_from, values, left):
                    turned()
                    hold(held_from, values[:, 0, 0:1])
                    for b in range(QUAD):
                        last = V.max(out16[:, b, 0:8], values[:, b, :])
                    did(last)
                    turned()
                    hold(held_from + 1, out16[:, 0, 0:1])
                    for b in range(QUAD):
                        last = V.match_replace(left[:, b, :], out16[:, b, 0:8], values[:, b, :], 0.0)
                    did(last)
                    turned()
                    hold(held_from + 2, left[:, 0, 0:1])
                    for b in range(QUAD):
                        last = V.max(out16[:, b, 8:16], left[:, b, :])
                    did(last)
                    turned()

                key(0)
                key(1)
                search(0)
                key(2)
                search(1)
                key(3)
                search(2)
                did(search(3))
                greatest16(top16, 4, found[:, 0, :, :], found[:, 1, :, :])
                whole, f_bits, product, column = (key_i[:, i, :, :] for i in range(4))
                f_least, f_inverse, quotient = (key_f[:, i, :, :] for i in range(3))
                did(V.tensor_copy(whole, top16[:, :, :])); turned()
                did(V.tensor_single_scalar(f_bits, whole, KEY_SHIFT, op=ALU.logical_shift_right))
                did(V.tensor_single_scalar(product, whole, (1 << KEY_SHIFT) - 1, op=ALU.bitwise_and)); turned()
                did(V.tensor_scalar_max(f_least, f_bits, 1.0)); turned()
                did(V.reciprocal(f_inverse, f_least))
                for k in range(FOLDS):
                    did(V.tensor_scalar(bits[:, k, :, :], f_bits, k, 1, ALU.logical_shift_right, ALU.bitwise_and))
                turned()
                did(V.tensor_tensor(quotient, product, f_inverse, ALU.mult)); turned()
                did(V.tensor_scalar_add(column, quotient, 1.25)); turned()
                for k in range(FOLDS):
                    last = V.scalar_tensor_tensor(edge[:, :, k, :], column, float(k * FOLDED), bits[:, k, :, :], ALU.add, ALU.mult)
                did(last)
                edges = edge[:, :, :, :].rearrange("p b k s -> p b (k s)")
                greatest16(top16, 8, edges, edge_left)
                did(V.tensor_copy(record_i[:, bass.ds(quad * QUAD, QUAD), C_NBR:C_NBR + SLOTS], top16[:, :, :])); turned()
                assert now == QUAD_STEPS, now
            after()
            do(V.tensor_single_scalar(held[:, :, :], record_i[:, :, C_NBR:C_NBR + SLOTS], 0.0, op=ALU.is_gt)); after()
            deg = record[:, :, C_DEG]
            do(V.tensor_reduce(deg, held[:, :, :], AX.X, ALU.add)); after()
            dve.wait_ge(masked, T)
            do(V.tensor_tensor(small[:, 0, :], row_sum[:, :], deg, ALU.is_equal)); after()
            do(V.scalar_tensor_tensor(small[:, 1, :], deg, float(-(SLOTS + 1)), small[:, 0, :], ALU.add, ALU.mult)); after()
            do(V.tensor_scalar_add(small[:, 2, :], small[:, 1, :], float(SLOTS + 1))); after()
            dve.wait_ge(pool_made, 6)
            V.tensor_tensor(onehot[:, :, :], level_of[:, :, :], small[:, 2, :].unsqueeze(1).to_broadcast([P, LEVELS, T]),
                            ALU.is_equal).then_inc(onehot_made, 1)
            dve.wait_ge(counted, 1)
            half = LEVELS // 2
            for b in range(2):
                sl = slice(b * half, (b + 1) * half)
                do(V.tensor_copy(total[:, sl, :], ps_tot[b][:, 0:half * T].rearrange("p (l t) -> p l t", t=T)))
                do(V.tensor_copy(pre[0][:, sl, PAD:], ps_tot[b][:, 0:half * T].rearrange("p (l t) -> p l t", t=T)))
            after()
            cur = 0
            for shift in (1, 2, 4, 8, 16):
                do(V.tensor_tensor(pre[1 - cur][:, :, PAD:], pre[cur][:, :, PAD:], pre[cur][:, :, PAD - shift:PAD - shift + T], ALU.add)); after()
                cur = 1 - cur
            tiles_incl = pre[cur]
            do(V.tensor_copy(lev[0][:, PAD:], tiles_incl[:, :, PAD + T - 1])); after()
            cur = 0
            for shift in (1, 2, 4, 8, 16):
                do(V.tensor_tensor(lev[1 - cur][:, PAD:], lev[cur][:, PAD:], lev[cur][:, PAD - shift:PAD - shift + LEVELS], ALU.add)); after()
                cur = 1 - cur
            levels_incl = lev[cur]
            dve.wait_ge(pool_made, POOL_MADE)
            do(V.tensor_tensor(over[:, 0:LEVELS - 1], levels_incl[:, PAD:PAD + LEVELS - 1], caps[:, :], ALU.is_gt))
            do(V.tensor_single_scalar(over[:, LEVELS - 1:LEVELS], levels_incl[:, PAD + LEVELS - 2:PAD + LEVELS - 1], float(N - P), op=ALU.is_lt))
            after()
            do(V.tensor_reduce(flag_f[:, :], over[:, :], AX.X, ALU.add)); after()
            do(V.tensor_copy(flag_i[:, :], flag_f[:, :])); after()
            do(V.tensor_tensor(place[:, :, :], tiles_incl[:, :, PAD:], total[:, :, :], ALU.subtract))
            do(V.tensor_tensor(lev[1 - cur][:, PAD:], levels_incl[:, PAD:], tiles_incl[:, :, PAD + T - 1], ALU.subtract)); after()
            do(V.tensor_tensor(place[:, :, :], place[:, :, :], lev[1 - cur][:, PAD:].unsqueeze(2).to_broadcast([P, LEVELS, T]), ALU.add)); after()
            for b in range(2):
                sl = slice(b * half, (b + 1) * half)
                do(V.tensor_tensor(place[:, sl, :], place[:, sl, :], ps_lt[b][:, 0:half * T].rearrange("p (l t) -> p l t", t=T), ALU.add))
            after()
            do(V.tensor_tensor(total[:, :, :], place[:, :, :], onehot[:, :, :], ALU.mult)); after()
            do(V.tensor_reduce(small[:, 3, :], total[:, :, :].rearrange("p l t -> p t l"), AX.X, ALU.add)); after()
            V.tensor_copy(rank_i[:, :], small[:, 3, :]).then_inc(ranks_made, 1)
            V.tensor_scalar_add(record[:, :, C_RANK], small[:, 3, :], 1.0).then_inc(ranks_made, 1)
            dve.wait_ge(score_copied, 1)
            V.tensor_reduce(best_dst[:, 0:1], record[:, :, C_SDST], AX.X, ALU.max).then_inc(tops_made, 1)
            V.engine_nop().then_inc(flag_made, 1)
            big_degree = dve.value_load(flag_i[0:1, 0:1], min_val=0, max_val=64)
            with dve.If(big_degree == 0):
                LAST = T - 1

                def bc(ap, shape, axis):
                    return ap.unsqueeze(axis).to_broadcast(shape)

                dve.wait_ge(lists_loaded, 16)
                dve.wait_ge(best_made, 1)
                V.tensor_scalar(diag[:, :], ident[:, :], ranked[:, LAST, C_SSRC:C_SSRC + 1], None, ALU.mult).then_inc(diag_made, 1)
                do(V.tensor_single_scalar(has_nbr[:, :], ranked[:, :, C_DEG], 0.0, op=ALU.is_gt)); after()
                do(V.tensor_scalar(no_nbr[:, :], has_nbr[:, :], -1.0, 1.0, ALU.mult, ALU.add))
                dve.wait_ge(src_spread, 1)
                src_row = ps_small[:, 128:256]
                do(V.tensor_scalar_add(row_max[:, 0, :], src_row, best_dst[:, 1:2])); after()
                do(V.scalar_tensor_tensor(row_max[:, 1, :], row_max[:, 0, :], SLOPE, row_max[:, 0, :], ALU.mult, ALU.max)); after()
                do(V.tensor_scalar_add(row_max[:, 0, :], row_max[:, 1, :], MASKED)); after()
                flat = big[:, 0, 0:T * F]
                do(V.tensor_tensor(weights_t, bc(src_row, [P, T, P], 1), bc(record[:, :, C_SDST], [P, T, P], 2), ALU.add)); after()
                do(V.scalar_tensor_tensor(flat, flat, SLOPE, flat, ALU.mult, ALU.max)); after()
                do(V.tensor_scalar_add(flat, flat, MASKED)); after()
                V.tensor_tensor(weights_t, weights_t, bc(row_max[:, 0, :], [P, T, P], 1), ALU.subtract).then_inc(lone_scored, 1)

                norms = 0

                def y_free(layer, g):
                    if g >= 2:
                        dve.wait_ge(layer_done[layer], g - 1)
                    elif layer:
                        dve.wait_ge(layer_done[layer - 1], len(GROUPS))

                def norm(layer, g):
                    n = GROUPS[g][1]
                    nonlocal norms
                    for i in range(n):
                        do(V.bn_stats(moments[:, i, :], y[:, g % 2, i, :]))
                    after()
                    for i in range(n):
                        do(V.bn_aggr(mean_var[:, i, :], moments[:, i, :]))
                    after()
                    V.tensor_scalar_add(stat[:, 5, 0:n], mean_var[:, 0:n, 1], EPS).then_inc(variance_ready, 1)
                    norms += 1
                    dve.wait_ge(deviation_ready, norms)
                    do(V.reciprocal(norm_scale[:, g % 2, 0:n], stat[:, 6, 0:n])); after()
                    V.scalar_tensor_tensor(norm_shift[:, g % 2, 0:n], mean_var[:, 0:n, 0], -1.0, norm_scale[:, g % 2, 0:n],
                                           ALU.mult, ALU.mult).then_inc(shift_ready, 1)

                def attention(layer, width, s_src, first):
                    def scores(g):
                        t0, n, depth, s0 = GROUPS[g]
                        dve.wait_ge(gathered[g], 16 * n * depth * (layer + 1))
                        rows = gat(width, s0, n * depth).rearrange("p (t k f) -> p t k f", t=n, k=depth)
                        z = score[:, g % 2, 0:n * depth]
                        z3 = z.rearrange("p (t k) -> p t k", t=n)
                        do(V.tensor_tensor(z3, rows[:, :, :, C_SDST], bc(s_src[:, t0:t0 + n], [P, n, depth], 2), ALU.add)); after()
                        if layer == 0:
                            do(V.tensor_copy(nbr_rank[:, s0:s0 + n * depth].rearrange("p (t k) -> p t k", t=n), rows[:, :, :, C_RANK]))
                        do(V.scalar_tensor_tensor(z, z, SLOPE, z, ALU.mult, ALU.max)); after()
                        do(V.tensor_reduce(stat[:, g % 2, 0:n], z3, AX.X, ALU.max)); after()
                        V.tensor_tensor(z3, z3, bc(stat[:, g % 2, 0:n], [P, n, depth], 2), ALU.subtract).then_inc(scores_ready, 1)

                    def weigh(g):
                        t0, n, depth, s0 = GROUPS[g]
                        dve.wait_ge(exps_ready, first + g + 1)
                        rows = gat(width, s0, n * depth).rearrange("p (s f) -> p s f", f=width)[:, :, 0:F]
                        p2 = score[:, g % 2, 0:n * depth]
                        do(V.tensor_reduce(stat[:, 2, 0:n], p2.rearrange("p (t k) -> p t k", t=n), AX.X, ALU.add))
                        sums = steps
                        y_free(layer, g)
                        for k in range(depth):
                            for i in range(n):
                                s = i * depth + k
                                if k:
                                    after(steps - n + 1)
                                    do(V.scalar_tensor_tensor(y[:, g % 2, i, :], rows[:, s, :], p2[:, s:s + 1], y[:, g % 2, i, :], ALU.mult, ALU.add))
                                else:
                                    do(V.tensor_scalar(y[:, g % 2, i, :], rows[:, s, :], p2[:, s:s + 1], None, ALU.mult))
                            if k == 0:
                                after(sums)
                                do(V.reciprocal(stat[:, 3, 0:n], stat[:, 2, 0:n]))
                        after()
                        for i in range(n):
                            do(V.scalar_tensor_tensor(y[:, g % 2, i, :], y[:, g % 2, i, :], stat[:, 3, i:i + 1], ranked[:, t0 + i, 0:F], ALU.mult, ALU.add))
                        after()
                        if t0 + n == T:
                            i = n - 1
                            do(V.scalar_tensor_tensor(y[:, g % 2, i, :], (lone if layer == 0 else h_mean)[:, :], no_nbr[:, LAST:T],
                                                      y[:, g % 2, i, :], ALU.mult, ALU.add)); after()
                        norm(layer, g)

                    for g in range(len(GROUPS)):
                        scores(g)
                        if GROUPS[g][0] + GROUPS[g][1] == T and layer == 0:
                            dve.wait_ge(lone_summed, 1)
                            do(V.reciprocal(lone_sum[:, :], ps_small[:, 256:257])); after()
                            do(V.tensor_scalar(lone[:, :], ps_acc[:, 0:F], lone_sum[:, :], None, ALU.mult)); after()
                        weigh(g)

                def neighbour_max(layer):
                    for g, (t0, n, depth, s0) in enumerate(GROUPS):
                        dve.wait_ge(gathered[g], 16 * n * depth * (layer + 1))
                        rows = gat(F, s0, n * depth).rearrange("p (t k f) -> p t f k", t=n, k=depth)
                        own = ranked[:, t0:t0 + n, 0:F]
                        y_free(layer, g)
                        if depth > 1:
                            do(V.tensor_reduce(y[:, g % 2, 0:n, :], rows, AX.X, ALU.max)); after()
                            do(V.tensor_tensor(y[:, g % 2, 0:n, :], y[:, g % 2, 0:n, :], own, ALU.add)); after()
                        else:
                            for i in range(n):
                                do(V.scalar_tensor_tensor(y[:, g % 2, i, :], rows[:, i, :, 0], has_nbr[:, t0 + i:t0 + i + 1],
                                                          ranked[:, t0 + i, 0:F], ALU.mult, ALU.add))
                            after()
                        norm(layer, g)

                dve.wait_ge(x_ranked, 16)
                attention(0, W0, ranked[:, :, C_SSRC], 0)
                neighbour_max(1)
                neighbour_max(2)
                dve.wait_ge(mean_made, 1)
                do(V.tensor_copy(h_mean[:, :], ps_acc[:, 128:128 + F])); after()
                attention(3, W3, h[:, :, F + 1], len(GROUPS))
            with dve.Else():
                for layer in range(4):
                    d = DENSE[layer]

                    turn_steps = 0

                    def did(ins):
                        nonlocal turn_steps
                        turn_steps += 1
                        ins.then_inc(d["step"], 1)

                    def turned(t):
                        dve.wait_ge(d["step"], t * STEPS[layer] + turn_steps)

                    def finish(t, agg, scale):
                        did(V.tensor_copy(d_own[:, :], record[:, bass.ds(t, 1), 0:F].rearrange("p a f -> p (a f)"))); turned(t)
                        if scale is None:
                            did(V.tensor_tensor(d_y[:, 0, :], agg, d_own[:, :], ALU.add)); turned(t)
                        else:
                            did(V.scalar_tensor_tensor(d_y[:, 0, :], agg, scale, d_own[:, :], ALU.mult, ALU.add)); turned(t)
                        did(V.bn_stats(d_mom[:, :], d_y[:, 0, :])); turned(t)
                        did(V.tensor_copy(d_col[:, 6:7], d_mom[:, 0:1]))
                        did(V.bn_aggr(d_mv[:, :], d_mom[:, :])); turned(t)
                        V.tensor_scalar_add(d_col[:, 3:4], d_mv[:, 1:2], EPS).then_inc(d["var"], 1)
                        dve.wait_ge(d["dev"], t + 1)
                        did(V.reciprocal(d_col[:, 5:6], d_col[:, 4:5])); turned(t)
                        did(V.tensor_scalar(d_y[:, 1, :], d_y[:, 0, :], d_mv[:, 0:1], d_col[:, 5:6], ALU.subtract, ALU.mult)); turned(t)
                        assert turn_steps == STEPS[layer], (layer, turn_steps)

                    if layer:
                        dve.wait_ge(d["x_in"], 16)
                    if layer in (0, 3):
                        if layer == 0:
                            dve.wait_ge(ranks_made, 2)
                            dve.wait_ge(score_copied, 1)
                            V.tensor_copy(ranked[:, :, 0:W0], record[:, :, 0:W0]).then_inc(d["v_ready"], 1)
                        dve.wait_ge(d["v_ready"], 1 if layer == 0 else T)
                        dve.wait_ge(d["dst_in"], 16)
                        with dve.Fori(0, T) as t:
                            turn_steps = 0
                            did(V.tensor_copy(d_col[:, 0:1], ranked[:, bass.ds(t, 1), C_SSRC])); turned(t)
                            did(V.tensor_scalar(d_e, d_dst, d_col[:, 0:1], None, ALU.add)); turned(t)
                            did(V.scalar_tensor_tensor(d_e, d_e, SLOPE, d_e, ALU.mult, ALU.max))
                            dve.wait_ge(d["adj"], t * 16 + 16)
                            did(V.tensor_single_scalar(d_m, d_adj[0], 0.0, op=ALU.is_gt)); turned(t)
                            low = -MASKED if layer == 0 else 9e15
                            if layer == 3:
                                did(V.tensor_tensor(d_e, d_e, d_m, ALU.mult)); turned(t)
                            did(V.tensor_scalar(d_m, d_m, low, -low, ALU.mult, ALU.add)); turned(t)
                            did(V.tensor_tensor(d_e, d_e, d_m, ALU.add)); turned(t)
                            did(V.tensor_reduce(d_col[:, 1:2], d_e, AX.X, ALU.max, negate=True)); turned(t)
                            V.tensor_copy(d_col[:, 7:8], d_col[:, 1:2]).then_inc(d["score"], 1)
                            dve.wait_ge(d["exp"], t + 1)
                            did(V.reciprocal(d_col[:, 7:8], d_col[:, 2:3])); turned(t)
                            dve.wait_ge(d["acc"], t + 1)
                            finish(t, ps_acc[:, 0:F], d_col[:, 7:8])
                            dve.wait_ge(d["stored"], t * 16 + 16)
                    else:
                        dve.wait_ge(d["x_copied"], T // 4)
                        rows = (d["row_even"], d["row_odd"])
                        with dve.Fori(0, N // 2) as pair:
                            for b in range(2):
                                dve.wait_ge(rows[b], pair * 16 + 16)
                                V.tensor_scalar(d_e, d_adj[b], 0.0, LOWEST, ALU.is_equal, ALU.mult).then_inc(d["row_read"], 1)
                                dve.wait_ge(d["row_read"], pair * 2 + (b + 1))
                                V.tensor_reduce(d_has[:, bass.ds(pair * 2 + b, 1)], d_e, AX.X, ALU.max).then_inc(d["row_step"], 1)
                                V.tensor_tensor(d_m, d_e, d_xt, ALU.add).then_inc(d["row_step"], 1)
                                dve.wait_ge(d["row_step"], pair * 6 + (3 * b + 2))
                                V.tensor_reduce(d_max_t[:, bass.ds(pair * 2 + b, 1)], d_m, AX.X, ALU.max).then_inc(d["row_step"], 1)
                                dve.wait_ge(d["row_step"], pair * 6 + (3 * b + 3))
                        V.tensor_single_scalar(d_m, d_has, 0.0, op=ALU.is_equal).then_inc(d["row_read"], 1)
                        dve.wait_ge(d["row_read"], N + 1)
                        V.tensor_tensor(d_max_t, d_max_t, d_m, ALU.mult).then_inc(d["maxed"], 1)
                        with dve.Fori(0, T) as t:
                            turn_steps = 0
                            dve.wait_ge(d["back"], t + 1)
                            finish(t, ps_mm[0][:, 0:P], None)
                            dve.wait_ge(d["stored"], t * 16 + 16)


_INS = ["x", "adj", "L0_gnn_attn", "L3_gnn_W", "L3_gnn_a"]


def kernel(**inputs):
    import numpy as _np
    import concourse.bacc as _bacc
    from concourse import mybir as _mybir
    from concourse.bass_utils import run_bass_kernel_spmd as _run

    nc = _bacc.Bacc("TRN2", target_bir_lowering=False, num_devices=1)
    arrays, args = {}, []
    for name in _INS:
        a = _np.ascontiguousarray(inputs[name])
        arrays[f"in_{name}_dram"] = a
        args.append(nc.dram_tensor(f"in_{name}_dram", a.shape, _mybir.dt.from_np(a.dtype), kind="ExternalInput").ap())
    args.append(nc.dram_tensor("out_0_dram", (4096, 128), _mybir.dt.float32, kind="ExternalOutput").ap())
    gnn_kernel(nc, *args)
    r = _run(nc, [arrays], core_ids=[0])
    return r.results[0]["out_0_dram"]
```

```python
from contextlib import ExitStack

import concourse.bass as bass
from concourse import mybir

ALU = mybir.AluOpType
ACT = mybir.ActivationFunctionType
AX = mybir.AxisListType
F32 = mybir.dt.float32
BF16 = mybir.dt.bfloat16
I32 = mybir.dt.int32
U32 = mybir.dt.uint32
U16 = mybir.dt.uint16

P = 128
F = 128
N = 4096
T = N // P
SLOTS = 16
FOLDS = 4
FOLDED = N // FOLDS
SEARCHES = 8
KEY_SHIFT = 14
QUAD = 4
QUADS = T // QUAD
EPS = 1e-5
SLOPE = 0.2
MASKED = -1e9
LOWEST = -3.4028234663852886e38
FAR = -1e30

SERVED = [32, 30, 25, 19, 13, 8, 4, 2, 1]
PACKED = SLOTS - len(SERVED)
DEPTH = [sum(n > t for n in SERVED) for t in range(T)]
GATHERS = sum(DEPTH) + 1
_RUNS = [(25, 5), (19, 6), (0, 1), (13, 4), (30, 2), (8, 5), (17, 2), (4, 4), (2, 2), (1, 1)]
GROUPS = []
for _t, _n in _RUNS:
    assert len({DEPTH[_t + _i] for _i in range(_n)}) == 1
    GROUPS.append((_t, _n, DEPTH[_t], sum(n * k + (t == 0) for t, n, k, _ in GROUPS)))
assert (0, 1) in _RUNS
FIRST = _RUNS.index((0, 1))
assert sorted(t + i for t, n, _, _ in GROUPS for i in range(n)) == list(range(T))
BATCH = 3


def slots(g):
    return GROUPS[g][1] * GROUPS[g][2] + (g == FIRST)


def list_slots(g):
    return SLOTS if g == FIRST else GROUPS[g][2]


LEVELS = SLOTS + 2
STEPS = {0: 15, 1: 7, 2: 7, 3: 16}

C_SDST, C_RANK, C_SSRC, C_DEG, C_NBR, C_ID = F, F + 1, F + 2, F + 3, F + 4, F + 4 + SLOTS
RECORD = C_ID + 1
W0 = F + 4
W3 = F + 2


def gnn_kernel(nc, x, adj, attn, w, a3, out):
    with ExitStack() as ctx:
        def sb(name, shape, dt):
            return ctx.enter_context(nc.sbuf_tensor(name, shape, dt))

        def ps(name, shape, dt=F32):
            return ctx.enter_context(nc.psum_tensor(name, shape, dt))

        def sem(name):
            return ctx.enter_context(nc.semaphore(name))

        table0 = nc.dram_tensor("table0", [N + 1, W0], F32).ap()
        table1 = nc.dram_tensor("table1", [N + 1, F], F32).ap()
        table2 = nc.dram_tensor("table2", [N + 1, F], F32).ap()
        table3 = nc.dram_tensor("table3", [N + 1, W3], F32).ap()
        ranked_dram = nc.dram_tensor("ranked_dram", [N, RECORD], F32).ap()
        dense_dram = [nc.dram_tensor(f"dense_dram{i}", [N, F], F32).ap() for i in range(3)]
        dst_dram = {i: nc.dram_tensor(f"dst_dram{i}", [N], F32).ap() for i in (0, 3)}

        work = sb("work", [P, GATHERS * W0], F32)
        adj_buf = [work[:, b * N:(b + 1) * N].bitcast(I32) for b in range(QUAD)]
        column_w = sb("column_w", [P, FOLDED], F32)
        fold_w = sb("fold_w", [P, FOLDS, P], BF16)
        record = sb("record", [P, T, RECORD], F32)
        record_i = record[:, :, :].bitcast(I32)
        ranked = sb("ranked", [P, T, RECORD], F32)
        ranked_i = ranked[:, :, :].bitcast(I32)
        big = sb("big", [P, 2, T * (F + 4)], F32)
        mask_buf = [big[:, b // 2, (b % 2) * (N // 2):(b % 2 + 1) * (N // 2)].bitcast(BF16) for b in range(QUAD)]
        key_buf = [ranked[:, :, :].rearrange("p t r -> p (t r)")[:, b * FOLDED:(b + 1) * FOLDED] for b in range(QUAD)]
        weights_t = big[:, 0, 0:T * F].rearrange("p (t i) -> p t i", t=T)
        h = big[:, 1, 0:T * W3].rearrange("p (t f) -> p t f", t=T)
        ident = sb("ident", [P, P], F32)
        ones = sb("ones", [P, P], F32)
        attn_cols = sb("attn_cols", [P, 2], F32)
        a3_cols = sb("a3_cols", [P, 2], F32)
        w_aug = sb("w_aug", [P, W3], F32)
        w_t = sb("w_t", [P, F], F32)
        x_t = sb("x_t", [P, 2, 4 * P], F32)
        empty = sb("empty", [1, 4, W0], F32)
        found = sb("found", [P, 2, QUAD, 64], F32)
        top16 = sb("top16", [P, QUAD, SLOTS], F32)
        edge = sb("edge", [P, QUAD, FOLDS, SLOTS], F32)
        edge_left = sb("edge_left", [P, QUAD, FOLDS * SLOTS], F32)
        key_i = sb("key_i", [P, 4, QUAD, SLOTS], I32)
        key_f = sb("key_f", [P, 3, QUAD, SLOTS], F32)
        bits = sb("bits", [P, FOLDS, QUAD, SLOTS], I32)
        held_word = sb("held_word", [P, 16], F32)
        row_sum = sb("row_sum", [P, T], F32)
        low_bf = sb("low_bf", [P, P], BF16)
        ones_bf = sb("ones_bf", [P, P], BF16)
        minus_bf = sb("minus_bf", [P, P], BF16)
        held = sb("held", [P, QUAD, SLOTS], F32)
        quad_deg = sb("quad_deg", [P, 3, QUAD], F32)
        minus_level = sb("minus_level", [P, LEVELS + 1, QUAD], F32)
        PAD = QUAD - 1
        onehot = sb("onehot", [P, LEVELS, QUADS * (PAD + QUAD)], BF16)
        onehot_q = onehot[:, :, :].rearrange("p l (q j) -> p l q j", j=PAD + QUAD)
        below = sb("below", [P, LEVELS + 1, QUAD], F32)
        quad_below = sb("quad_below", [P, LEVELS + 1], F32)
        rows_below = sb("rows_below", [P, LEVELS + 1, QUADS + 1], BF16)
        place = sb("place", [P, LEVELS, T], F32)
        rank_f = sb("rank_f", [P, T], F32)
        rank_i = sb("rank_i", [P, T], I32)
        caps = sb("caps", [P, LEVELS - 1], F32)
        over = sb("over", [P, LEVELS + 1], F32)
        packed_rows = sb("packed_rows", [P, 1], F32)
        flag_f = sb("flag_f", [P, 1], F32)
        flag_i = sb("flag_i", [P, 1], I32)
        nbr_rank = sb("nbr_rank", [P, GATHERS], I32)
        maxn = max(n for _, n, _, _ in GROUPS)
        maxs = max(list_slots(g) * n for g, (_, n, _, _) in enumerate(GROUPS))
        score = sb("score", [P, 2, maxs], F32)
        stat = sb("stat", [P, 8, maxn], F32)
        y = sb("y", [P, 2, maxn, F], F32)
        norm_scale = sb("norm_scale", [P, 2, maxn], F32)
        norm_shift = sb("norm_shift", [P, 2, maxn], F32)
        moments = sb("moments", [P, maxn, 6], F32)
        mean_var = sb("mean_var", [P, maxn, 2], F32)
        pack_start = sb("pack_start", [P, PACKED + 1], F32)
        lane_minus_row = sb("lane_minus_row", [P, P], F32)
        lane_minus_row_t = sb("lane_minus_row_t", [P, P], F32)
        to_lane = sb("to_lane", [P, PACKED, P], F32)
        to_row = sb("to_row", [P, PACKED, P], F32)
        in_part = sb("in_part", [P, 3, PACKED], F32)
        packed_nbr = sb("packed_nbr", [P, PACKED], F32)
        missing = sb("missing", [P, 3, PACKED], F32)
        packed_index = sb("packed_index", [P, 1], I32)
        odd_slots = sb("odd_slots", [P, F], F32)
        has_nbr = sb("has_nbr", [P, T], F32)
        no_nbr = sb("no_nbr", [P, T], F32)
        best_dst = sb("best_dst", [P, 2], F32)
        diag = sb("diag", [P, P], F32)
        row_max = sb("row_max", [P, 2, P], F32)
        lone = sb("lone", [P, F], F32)
        lone_sum = sb("lone_sum", [P, 1], F32)
        h_mean = sb("h_mean", [P, F], F32)
        x3_t = sb("x3_t", [P, 2, BATCH * P], F32)
        mean_w = sb("mean_w", [P, P], F32)

        d_adj = [work[:, b * N:(b + 1) * N].bitcast(I32) for b in range(2)]
        d_e = work[:, 2 * N:3 * N]
        d_m = work[:, 3 * N:4 * N]
        d_dst = big[:, 0, 0:N]
        d_xt = big[:, 0, 0:N]
        d_pt = big[:, 1, 0:N]
        d_max_t = big[:, 1, 0:N]
        d_has = ranked[:, :, :].rearrange("p t r -> p (t r)")[:, 0:N]
        d_y = sb("d_y", [P, 2, F], F32)
        d_own = sb("d_own", [P, F], F32)
        d_col = sb("d_col", [P, 8], F32)
        d_mom = sb("d_mom", [P, 6], F32)
        d_mv = sb("d_mv", [P, 2], F32)

        ps_fold = [ps(f"ps_fold{b}", [P, FOLDED]) for b in range(2)]
        ps_tr = [ps_fold[0][:, b * 512:(b + 1) * 512] for b in range(2)]
        ps_mm = [ps_fold[1][:, b * 512:(b + 1) * 512] for b in range(2)]
        ps_small = ps("ps_small", [P, 512])
        ps_acc = ps("ps_acc", [P, 512])
        ps_x = [ps(f"ps_x{b}", [P, 4 * P]) for b in range(2)]
        ps_place = [ps_tr[0], ps_tr[1], ps_mm[0]]
        ps_below = ps_mm[1][:, 0:LEVELS + 1]

        ps_unpack = [ps_x[0], ps_x[1], ps_small[:, 264:512]]
        ps_packed = ps_small[:, 262:263]

        def unpacked_row(k, width):
            return ps_unpack[k // 3][:, (k % 3) * width:(k % 3 + 1) * width]

        adj_loaded = [sem(f"adj_loaded{b}") for b in range(QUAD)]
        masked = sem("masked")
        folded = sem("folded")
        keyed = sem("keyed")
        searched = sem("searched")
        attn_loaded = sem("attn_loaded")
        w_loaded = sem("w_loaded")
        x_loaded = sem("x_loaded")
        pool_made = sem("pool_made")
        x_transposed = sem("x_transposed")
        xt_copied = sem("xt_copied")
        scored = sem("scored")
        score_copied = sem("score_copied")
        w_turned = sem("w_turned")
        wt_copied = sem("wt_copied")
        wa_made = sem("wa_made")
        wa_copied = sem("wa_copied")
        dve_step = sem("dve_step")
        counted = sem("counted")
        ranks_made = sem("ranks_made")
        flag_made = sem("flag_made")
        tops_made = sem("tops_made")
        best_made = sem("best_made")
        empty_written = sem("empty_written")
        table0_written = sem("table0_written")
        scattered = sem("scattered")
        lists_loaded = sem("lists_loaded")
        x_ranked = sem("x_ranked")
        gathered = [sem(f"gathered{g}") for g in range(len(GROUPS))]
        scores_ready = sem("scores_ready")
        exps_ready = sem("exps_ready")
        variance_ready = sem("variance_ready")
        shift_ready = sem("shift_ready")
        deviation_ready = sem("deviation_ready")
        pack_made = sem("pack_made")
        packed = sem("packed")
        packed_ready = sem("packed_ready")
        unpacked = sem("unpacked")
        diag_made = sem("diag_made")
        src_spread = sem("src_spread")
        lone_scored = sem("lone_scored")
        lone_exp = sem("lone_exp")
        lone_summed = sem("lone_summed")
        layer_done = [sem(f"layer{i}_done") for i in range(4)]
        table_written = {i: sem(f"table{i}_written") for i in (1, 2, 3)}
        x3_turned = sem("x3_turned")
        x3t_copied = sem("x3t_copied")
        h_made = sem("h_made")
        h_copied = sem("h_copied")
        mean_made = sem("mean_made")
        out_written = sem("out_written")
        DENSE = {}
        for layer in range(4):
            names = ["x_in", "step", "dev", "var", "stored"]
            if layer in (0, 3):
                names += ["v_ready", "dst_out", "dst_in", "adj", "score", "exp", "turned", "copied", "acc"]
            if layer == 3:
                names += ["x_turned", "x_copied", "h_made"]
            if layer in (1, 2):
                names += ["x_turned", "x_copied", "row_even", "row_odd", "row_read", "row_step", "maxed", "back"]
            DENSE[layer] = {k: sem(f"dense{layer}_{k}") for k in names}

        block = ctx.enter_context(nc.Block())

        QUAD_STEPS = 29
        POOL_MADE = 15 + (LEVELS - 1) + 2 * FOLDS

        batches, made_so_far = [], 0
        for t0, n, _, _ in GROUPS:
            starts = range(0, n, BATCH)
            batches.append([(made_so_far + j, t0 + i, min(BATCH, n - i)) for j, i in enumerate(starts)])
            made_so_far += len(starts)

        def gat(width, slot, count):
            return work[:, slot * width:(slot + count) * width]

        @block.sync
        def _(sp):
            for b in range(QUAD):
                sp.dma_start(adj_buf[b], adj[b * P:(b + 1) * P, :]).then_inc(adj_loaded[b], 16)
            with sp.Fori(0, QUADS - 1) as quad:
                for b in range(QUAD):
                    sp.wait_ge(masked, quad * QUAD + (b + 1))
                    sp.dma_start(adj_buf[b], adj[bass.ds(quad * (QUAD * P) + (QUAD + b) * P, P), :]).then_inc(adj_loaded[b], 16)
            sp.dma_start(record[:, :, 0:F], x.rearrange("(t p) f -> p t f", p=P)).then_inc(x_loaded, 16)
            sp.wait_ge(ranks_made, 2)
            sp.wait_ge(score_copied, 1)
            sp.wait_ge(x_loaded, 16)
            sp.dma_start(table0[1:N + 1, :].rearrange("(t p) f -> p t f", p=P),
                         record[:, :, 0:W0]).then_inc(table0_written, 16)
            sp.wait_ge(flag_made, 1)
            big_degree = sp.value_load(flag_i[0:1, 0:1], min_val=0, max_val=64)
            with sp.If(big_degree == 0):
                sp.wait_ge(scattered, 16 * T)
                sp.dma_start(ranked[:, :, C_SDST:RECORD],
                             ranked_dram.rearrange("(t p) f -> p t f", p=P)[:, :, C_SDST:RECORD]).then_inc(lists_loaded, 16)
                for layer, table, width in ((1, table1, F), (2, table2, F)):
                    for g, (t0, n, _, _) in enumerate(GROUPS):
                        sp.wait_ge(layer_done[layer - 1], g + 1)
                        sp.dma_start(table[1 + t0 * P:1 + (t0 + n) * P, :].rearrange("(t p) f -> p t f", p=P),
                                     ranked[:, t0:t0 + n, 0:F]).then_inc(table_written[layer], 16)
                for g, (t0, n, _, _) in enumerate(GROUPS):
                    sp.wait_ge(h_copied, batches[g][-1][0] + 1)
                    sp.dma_start(table3[1 + t0 * P:1 + (t0 + n) * P, :].rearrange("(t p) f -> p t f", p=P),
                                 h[:, t0:t0 + n, :]).then_inc(table_written[3], 16)
            with sp.Else():
                for layer in range(4):
                    d = DENSE[layer]
                    to = out if layer == 3 else dense_dram[layer]
                    if layer:
                        sp.wait_ge(table0_written, 16)
                        sp.wait_ge(DENSE[layer - 1]["stored"], 16 * T)
                        sp.dma_start(record[:, :, 0:F], dense_dram[layer - 1].rearrange("(t p) f -> p t f", p=P)).then_inc(d["x_in"], 16)
                    if layer in (0, 3):
                        sp.wait_ge(d["v_ready"], 1 if layer == 0 else T)
                        sp.dma_start(dst_dram[layer].rearrange("(t p) -> p t", p=P), ranked[:, :, C_SDST],
                                     allow_slow_non_contiguous=True).then_inc(d["dst_out"], 16)
                        sp.wait_ge(d["dst_out"], 16)
                        sp.dma_start(d_dst, dst_dram[layer].partition_broadcast(P)).then_inc(d["dst_in"], 16)
                        with sp.Fori(0, T) as t:
                            sp.dma_start(d_adj[0], adj[bass.ds(t * P, P), :]).then_inc(d["adj"], 16)
                            sp.wait_ge(d["step"], t * STEPS[layer] + STEPS[layer])
                            sp.dma_start(to[bass.ds(t * P, P), :], d_y[:, 1, :]).then_inc(d["stored"], 16)
                    else:
                        rows = (d["row_even"], d["row_odd"])
                        for b in range(2):
                            sp.dma_start(d_adj[b], adj[b, :].partition_broadcast(P)).then_inc(rows[b], 16)
                        with sp.Fori(0, N // 2 - 1) as pair:
                            for b in range(2):
                                sp.wait_ge(d["row_read"], pair * 2 + (b + 1))
                                sp.dma_start(d_adj[b], adj[bass.ds(pair * 2 + (2 + b), 1), :].rearrange("a n -> (a n)").partition_broadcast(P)).then_inc(rows[b], 16)
                        with sp.Fori(0, T) as t:
                            sp.wait_ge(d["step"], t * STEPS[layer] + STEPS[layer])
                            sp.dma_start(to[bass.ds(t * P, P), :], d_y[:, 1, :]).then_inc(d["stored"], 16)
                sp.wait_ge(DENSE[3]["stored"], 16 * T)

        @block.gpsimd
        def _(pool):
            made = 0

            def make(ins):
                nonlocal made
                made += 1
                ins.then_inc(pool_made, 1)
                return made

            make(nc.gpsimd.iota(column_w[:, :], pattern=[[1, FOLDED]], base=1 << KEY_SHIFT, channel_multiplier=0,
                                allow_small_or_imprecise_dtypes=True))
            make(nc.gpsimd.memset(ones[:, :], 1.0))
            pool.wait_ge(pool_made, made)
            make(nc.gpsimd.affine_select(out=ident[:, :], in_=ones[:, :], pattern=[[1, P]],
                                         compare_op=ALU.is_equal, fill=0.0, base=0, channel_multiplier=-1))
            make(nc.gpsimd.memset(ones_bf[:, :], 1.0))
            pool.wait_ge(pool_made, made)
            make(nc.gpsimd.affine_select(out=low_bf[:, :], in_=ones_bf[:, :], pattern=[[1, P]],
                                         compare_op=ALU.is_gt, fill=0.0, base=0, channel_multiplier=-1))
            make(nc.gpsimd.iota(minus_level[:, :, :], pattern=[[-1, LEVELS + 1], [0, QUAD]], base=0,
                                channel_multiplier=0, allow_small_or_imprecise_dtypes=True))
            make(nc.gpsimd.iota(record_i[:, :, C_ID], pattern=[[P, T]], base=0, channel_multiplier=1))
            make(nc.gpsimd.iota(lane_minus_row[:, :], pattern=[[1, P]], base=0, channel_multiplier=-1,
                                allow_small_or_imprecise_dtypes=True))
            make(nc.gpsimd.iota(lane_minus_row_t[:, :], pattern=[[-1, P]], base=0, channel_multiplier=1,
                                allow_small_or_imprecise_dtypes=True))
            make(nc.gpsimd.memset(minus_bf[:, :], -1.0))
            make(nc.gpsimd.memset(mean_w[:, :], 1.0 / N))
            make(nc.gpsimd.memset(empty[:, :, :], 0.0))
            pool.wait_ge(pool_made, made)
            make(nc.gpsimd.memset(empty[:, 0, C_SDST:C_SDST + 1], FAR))
            make(nc.gpsimd.memset(empty[:, 1, :], LOWEST))
            make(nc.gpsimd.memset(empty[:, 3, C_SDST:C_SDST + 1], FAR))
            make(nc.gpsimd.memset(caps[:, 0:1], 0.0))
            for level in range(1, LEVELS - 1):
                make(nc.gpsimd.memset(caps[:, level:level + 1], float(P * (SERVED[SLOTS - level] if SLOTS - level < len(SERVED) else 1))))
            for k in range(FOLDS):
                make(nc.gpsimd.memset(fold_w[:, k, :], float(1 << k)))
            pool.wait_ge(pool_made, made)
            for k in range(FOLDS):
                make(nc.gpsimd.affine_select(out=fold_w[:, k, :], in_=fold_w[:, k, :], pattern=[[1, P]],
                                             compare_op=ALU.is_equal, fill=0.0, base=0, channel_multiplier=-1))
            assert made == POOL_MADE
            pool.wait_ge(tops_made, 1)
            nc.gpsimd.partition_all_reduce(best_dst[:, 1:2], best_dst[:, 0:1], P,
                                           bass.bass_isa.ReduceOp.max).then_inc(best_made, 1)
            pool.wait_ge(flag_made, 1)
            big_degree = pool.value_load(flag_i[0:1, 0:1], min_val=0, max_val=64)
            with pool.If(big_degree == 0):
                pool.wait_ge(ranks_made, 2)
                pool.wait_ge(score_copied, 1)
                pool.wait_ge(x_loaded, 16)
                for t in range(T):
                    pool.indirect_dma_start(out=ranked_dram, out_offset=bass.IndirectOffsetOnAxis(ap=rank_i[:, t:t + 1], axis=0),
                                            in_=record[:, t, :], in_offset=None).then_inc(scattered, 16)
                pool.wait_ge(lists_loaded, 16)
                pool.wait_ge(table0_written, 16)
                pool.wait_ge(empty_written, 16 * 4)

                def gather(table, width, index, packed_at):
                    for g, (t0, n, depth, s0) in enumerate(GROUPS):
                        def one(s, ap):
                            pool.indirect_dma_start(out=gat(width, s, 1), out_offset=None, in_=table,
                                                    in_offset=bass.IndirectOffsetOnAxis(ap=ap, axis=0)).then_inc(gathered[g], 16)

                        for t in range(t0, t0 + n):
                            for k in range(depth):
                                s = s0 + (t - t0) * depth + k
                                one(s, index(t, s, k))
                        if g == FIRST:
                            pool.wait_ge(packed_ready, 1)
                            one(s0 + depth, packed_at)

                packed_slot = GROUPS[FIRST][3] + GROUPS[FIRST][2]
                gather(table0, W0, lambda t, s, k: ranked_i[:, t, C_NBR + k:C_NBR + k + 1], packed_index[:, :])
                for layer, table, width in ((1, table1, F), (2, table2, F), (3, table3, W3)):
                    pool.wait_ge(layer_done[layer - 1], len(GROUPS))
                    pool.wait_ge(table_written[layer], 16 * len(GROUPS))
                    gather(table, width, lambda t, s, k: nbr_rank[:, s:s + 1], nbr_rank[:, packed_slot:packed_slot + 1])
                for g, (t0, n, _, _) in enumerate(GROUPS):
                    pool.wait_ge(layer_done[3], g + 1)
                    for t in range(t0, t0 + n):
                        pool.indirect_dma_start(out=out, out_offset=bass.IndirectOffsetOnAxis(ap=ranked_i[:, t, C_ID:C_ID + 1], axis=0),
                                                in_=ranked[:, t, 0:F], in_offset=None).then_inc(out_written, 16)
                pool.wait_ge(out_written, 16 * T)
            with pool.Else():
                pool.wait_ge(empty_written, 16 * 4)

        @block.scalar
        def _(act):
            act.dma_start(attn_cols[:, :], attn.rearrange("(c f) o -> f (c o)", f=F), allow_slow_non_contiguous=True).then_inc(attn_loaded, 16)
            act.dma_start(a3_cols[:, :], a3.rearrange("(c f) o -> f (c o)", f=F), allow_slow_non_contiguous=True).then_inc(w_loaded, 16)
            act.dma_start(w_aug[:, 0:F], w).then_inc(w_loaded, 16)
            act.wait_ge(pool_made, 15)
            act.dma_start(table0[0:1, :], empty[:, 0, :]).then_inc(empty_written, 16)
            act.dma_start(table1[0:1, :], empty[:, 1, 0:F]).then_inc(empty_written, 16)
            act.dma_start(table2[0:1, :], empty[:, 1, 0:F]).then_inc(empty_written, 16)
            act.dma_start(table3[0:1, :], empty[:, 3, 0:W3]).then_inc(empty_written, 16)

            def masks(quad, first):
                for b in range(QUAD):
                    act.wait_ge(adj_loaded[b], quad * 16 + 16)
                    if not first:
                        act.wait_ge(folded, quad * QUAD + (b + 1 - QUAD))
                    nc.scalar.activation(mask_buf[b], adj_buf[b].bitcast(U32), ACT.Copy,
                                         accum_out=row_sum[:, bass.ds(quad * QUAD + b, 1)]).then_inc(masked, 1)

            masks(0, True)
            with act.Fori(1, QUADS) as quad:
                masks(quad, False)
            act.wait_ge(w_turned, 1)
            nc.scalar.copy(w_t[:, :], ps_acc[:, 0:F]).then_inc(wt_copied, 1)
            act.wait_ge(wa_made, 1)
            nc.scalar.copy(w_aug[:, F:F + 1], ps_acc[:, P + 1:P + 2])
            nc.scalar.copy(w_aug[:, F + 1:F + 2], ps_acc[:, P:P + 1]).then_inc(wa_copied, 1)
            for q in range(T // 4):
                act.wait_ge(x_transposed, q + 1)
                if q >= 2:
                    act.wait_ge(scored, q - 1)
                nc.scalar.copy(x_t[:, q % 2, :], ps_x[q % 2][:, :]).then_inc(xt_copied, 1)
            act.wait_ge(scored, T // 4)
            scores = ps_small[:, 0:2 * T].rearrange("p (t c) -> p t c", c=2)
            nc.scalar.copy(record[:, :, C_SSRC], scores[:, :, 0])
            nc.scalar.copy(record[:, :, C_SDST], scores[:, :, 1]).then_inc(score_copied, 1)
            act.wait_ge(flag_made, 1)
            big_degree = act.value_load(flag_i[0:1, 0:1], min_val=0, max_val=64)
            with act.If(big_degree == 0):
                act.wait_ge(scattered, 16 * T)
                act.dma_start(ranked[:, :, 0:C_SDST],
                              ranked_dram.rearrange("(t p) f -> p t f", p=P)[:, :, 0:C_SDST]).then_inc(x_ranked, 16)

                G = len(GROUPS)

                def exponential(g, first):
                    values = score[:, g % 2, 0:GROUPS[g][1] * list_slots(g)]
                    act.wait_ge(scores_ready, first + g + 1)
                    nc.scalar.activation(values, values, ACT.Exp).then_inc(exps_ready, 1)

                def root(g, layer):
                    t0, n, _, _ = GROUPS[g]
                    act.wait_ge(variance_ready, layer * G + g + 1)
                    nc.scalar.activation(stat[:, 6, 0:n], stat[:, 5, 0:n], ACT.Sqrt).then_inc(deviation_ready, 1)
                    act.wait_ge(shift_ready, layer * G + g + 1)
                    for i in range(n):
                        last = nc.scalar.activation(ranked[:, t0 + i, 0:F], y[:, g % 2, i, :], ACT.Identity,
                                                    scale=norm_scale[:, g % 2, i:i + 1], bias=norm_shift[:, g % 2, i:i + 1])
                    last.then_inc(layer_done[layer], 1)

                def attention(first, layer):
                    for g in range(G):
                        exponential(g, first)
                        root(g, layer)

                act.wait_ge(lone_scored, 1)
                nc.scalar.activation(big[:, 0, 0:T * F], big[:, 0, 0:T * F], ACT.Exp).then_inc(lone_exp, 1)
                attention(0, 0)
                for layer in (1,):
                    for g in range(G):
                        root(g, layer)
                def h_copies(g):
                    for j, t, n in batches[g]:
                        act.wait_ge(x3_turned, j + 1)
                        nc.scalar.copy(x3_t[:, j % 2, 0:n * P], ps_tr[j % 2][:, 0:n * P]).then_inc(x3t_copied, 1)
                        act.wait_ge(h_made, j + 1)
                        nc.scalar.copy(h[:, t:t + n, :], ps_mm[j % 2][:, 0:n * W3].rearrange("p (t f) -> p t f", t=n)).then_inc(h_copied, 1)

                for g in range(G + 1):
                    if g < G:
                        root(g, 2)
                    if g >= 1:
                        h_copies(g - 1)
                attention(G, 3)
            with act.Else():
                for layer in range(4):
                    d = DENSE[layer]
                    if layer == 3:
                        with act.Fori(0, T) as t:
                            act.wait_ge(d["x_turned"], t + 1)
                            nc.scalar.copy(x3_t[:, 0, 0:P], ps_tr[0][:, 0:P]).then_inc(d["x_copied"], 1)
                            act.wait_ge(d["h_made"], t + 1)
                            nc.scalar.copy(ranked[:, bass.ds(t, 1), 0:F + 1], ps_mm[0][:, 0:F + 1].unsqueeze(1))
                            nc.scalar.copy(ranked[:, bass.ds(t, 1), C_SSRC], ps_mm[0][:, F + 1:F + 2]).then_inc(d["v_ready"], 1)
                    if layer in (0, 3):
                        with act.Fori(0, T) as t:
                            act.wait_ge(d["score"], t + 1)
                            nc.scalar.activation(d_e, d_e, ACT.Exp, bias=d_col[:, 1:2], accum_out=d_col[:, 2:3]).then_inc(d["exp"], 1)
                            for q in range(T // 4):
                                act.wait_ge(d["turned"], t * (T // 4) + (q + 1))
                                nc.scalar.copy(d_pt[:, q * 4 * P:(q + 1) * 4 * P], ps_tr[q % 2][:, :]).then_inc(d["copied"], 1)
                            act.wait_ge(d["var"], t + 1)
                            nc.scalar.activation(d_col[:, 4:5], d_col[:, 3:4], ACT.Sqrt).then_inc(d["dev"], 1)
                    else:
                        for q in range(T // 4):
                            act.wait_ge(d["x_turned"], q + 1)
                            nc.scalar.copy(d_xt[:, q * 4 * P:(q + 1) * 4 * P], ps_tr[q % 2][:, :]).then_inc(d["x_copied"], 1)
                        with act.Fori(0, T) as t:
                            act.wait_ge(d["var"], t + 1)
                            nc.scalar.activation(d_col[:, 4:5], d_col[:, 3:4], ACT.Sqrt).then_inc(d["dev"], 1)

        @block.tensor
        def _(pe):
            pe.wait_ge(pool_made, POOL_MADE)

            def fold(quad, first):
                for b in range(QUAD):
                    pe.wait_ge(masked, quad * QUAD + (b + 1))
                    if not (first and b < 2):
                        pe.wait_ge(keyed, quad * QUAD + (b - 1))
                    for c in range(0, FOLDED, 512):
                        for k in range(FOLDS):
                            last = nc.tensor.matmul(ps_fold[b % 2][:, c:c + 512], fold_w[:, k, :],
                                                    mask_buf[b][:, k * FOLDED + c:k * FOLDED + c + 512],
                                                    start=(k == 0), stop=(k == FOLDS - 1))
                    last.then_inc(folded, 1)

            fold(0, True)
            with pe.Fori(1, QUADS) as quad:
                fold(quad, False)
            pe.wait_ge(w_loaded, 32)
            nc.tensor.transpose(ps_acc[:, 0:F], w_aug[:, 0:F], ident[:, :]).then_inc(w_turned, 1)
            pe.wait_ge(wt_copied, 1)
            nc.tensor.matmul(ps_acc[:, P:P + 2], w_t[:, :], a3_cols[:, :], start=True, stop=True).then_inc(wa_made, 1)

            def score(q):
                pe.wait_ge(xt_copied, q + 1)
                for j in range(4):
                    last = nc.tensor.matmul(ps_small[:, 8 * q + 2 * j:8 * q + 2 * j + 2], x_t[:, q % 2, j * P:(j + 1) * P],
                                            attn_cols[:, :], start=True, stop=True)
                last.then_inc(scored, 1)

            pe.wait_ge(x_loaded, 16)
            pe.wait_ge(attn_loaded, 16)

            def x_steps(first, end):
                for q in range(first, end):
                    if q >= 2:
                        score(q - 2)
                    for j in range(4):
                        last = nc.tensor.transpose(ps_x[q % 2][:, j * P:(j + 1) * P], record[:, 4 * q + j, 0:F], ident[:, :])
                    last.then_inc(x_transposed, 1)

            x_steps(0, 4)
            def places(levels, quads, out):
                shape = [P, len(levels), len(quads), QUAD]
                l0, l1, q0, q1 = levels[0], levels[-1] + 1, quads[0], quads[-1] + 1
                to = out[:, 0:len(levels) * len(quads) * QUAD]

                def tiles(back):
                    return onehot_q[:, l0:l1, q0:q1, PAD - back:PAD - back + QUAD]

                nc.tensor.matmul(to, low_bf[:, :], tiles(0), start=True, stop=False)
                for back in range(1, QUAD):
                    nc.tensor.matmul(to, ones_bf[:, :], tiles(back), start=False, stop=False)
                nc.tensor.matmul(to, ones_bf[:, :], rows_below[:, l0 + 1:l1 + 1, q0:q1].unsqueeze(3).to_broadcast(shape), start=False, stop=False)
                nc.tensor.matmul(to, minus_bf[:, :], rows_below[:, l0:l1, q0:q1].unsqueeze(3).to_broadcast(shape), start=False, stop=False)

                def lower_levels():
                    return nc.tensor.matmul(to, ones_bf[:, :], rows_below[:, l0:l1, QUADS:QUADS + 1].unsqueeze(3).to_broadcast(shape), start=False, stop=True)
                return lower_levels

            half = LEVELS // 2
            pe.wait_ge(keyed, T)
            pe.wait_ge(searched, (QUADS - 1) * QUAD_STEPS)
            lower = [places(range(b * half, (b + 1) * half), range(QUADS - 1), ps_place[b]) for b in range(2)]
            x_steps(4, T // 4)
            score(T // 4 - 2)
            score(T // 4 - 1)
            pe.wait_ge(searched, QUADS * QUAD_STEPS)
            for last in lower:
                last()
            places(range(LEVELS), range(QUADS - 1, QUADS), ps_place[2])()
            nc.tensor.matmul(ps_below, ones_bf[:, :], rows_below[:, :, QUADS], start=True, stop=True).then_inc(counted, 1)
            pe.wait_ge(flag_made, 1)
            big_degree = pe.value_load(flag_i[0:1, 0:1], min_val=0, max_val=64)
            with pe.If(big_degree == 0):
                pe.wait_ge(pack_made, 1)
                for k in range(PACKED):
                    last = nc.tensor.matmul(ps_packed, to_lane[:, k, :], packed_nbr[:, k:k + 1], start=(k == 0), stop=(k == PACKED - 1))
                last.then_inc(packed, 1)

                def unpack(layer, width):
                    _, _, depth, s0 = GROUPS[FIRST]
                    if layer:
                        pe.wait_ge(layer_done[layer - 1], FIRST + 1)
                    pe.wait_ge(gathered[FIRST], 16 * slots(FIRST) * (layer + 1))
                    for k in range(PACKED):
                        last = nc.tensor.matmul(unpacked_row(k, width), to_row[:, k, :], gat(width, s0 + depth, 1), start=True, stop=True)
                    last.then_inc(unpacked, 1)

                pe.wait_ge(diag_made, 1)
                nc.tensor.matmul(ps_small[:, 128:256], ones[:, :], diag[:, :], start=True, stop=True).then_inc(src_spread, 1)
                pe.wait_ge(lone_exp, 1)
                for t in range(T):
                    nc.tensor.matmul(ps_acc[:, 0:F], weights_t[:, t, :], record[:, t, 0:F], start=(t == 0), stop=(t == T - 1))
                for t in range(T):
                    last = nc.tensor.matmul(ps_small[:, 256:257], weights_t[:, t, :], ones[:, 0:1], start=(t == 0), stop=(t == T - 1))
                last.then_inc(lone_summed, 1)
                unpack(0, W0)
                unpack(1, F)
                def mean(j, t, n):
                    pe.wait_ge(h_copied, j + 1)
                    for i in range(n):
                        last = nc.tensor.matmul(ps_acc[:, 128:128 + F], mean_w[:, :], h[:, t + i, 0:F],
                                                start=(j == 0 and i == 0), stop=(j == batches[-1][-1][0] and i == n - 1))
                    return last

                before = None
                for g in range(len(GROUPS)):
                    if g == FIRST - 1:
                        unpack(2, F)
                    pe.wait_ge(layer_done[2], g + 1)
                    for j, t, n in batches[g]:
                        for i in range(n):
                            last = nc.tensor.transpose(ps_tr[j % 2][:, i * P:(i + 1) * P], ranked[:, t + i, 0:F], ident[:, :])
                        last.then_inc(x3_turned, 1)
                        pe.wait_ge(x3t_copied, j + 1)
                        if j >= 2:
                            pe.wait_ge(h_copied, j - 1)
                        for i in range(n):
                            last = nc.tensor.matmul(ps_mm[j % 2][:, i * W3:(i + 1) * W3], x3_t[:, j % 2, i * P:(i + 1) * P], w_aug[:, :], start=True, stop=True)
                        last.then_inc(h_made, 1)
                        if before:
                            mean(*before)
                        before = j, t, n
                mean(*before).then_inc(mean_made, 1)
                unpack(3, W3)
            with pe.Else():
                for layer in range(4):
                    d = DENSE[layer]
                    if layer:
                        pe.wait_ge(d["x_in"], 16)
                    if layer == 3:
                        for t in range(T):
                            nc.tensor.transpose(ps_tr[0][:, 0:P], record[:, t, 0:F], ident[:, :]).then_inc(d["x_turned"], 1)
                            pe.wait_ge(d["x_copied"], t + 1)
                            nc.tensor.matmul(ps_mm[0][:, 0:W3], x3_t[:, 0, 0:P], w_aug[:, :], start=True, stop=True).then_inc(d["h_made"], 1)
                            pe.wait_ge(d["v_ready"], t + 1)
                    if layer in (0, 3):
                        with pe.Fori(0, T) as t:
                            pe.wait_ge(d["exp"], t + 1)
                            for q in range(T // 4):
                                if q >= 2:
                                    pe.wait_ge(d["copied"], t * (T // 4) + (q - 1))
                                for j in range(4):
                                    c = (4 * q + j) * P
                                    last = nc.tensor.transpose(ps_tr[q % 2][:, j * P:(j + 1) * P], d_e[:, c:c + P], ident[:, :])
                                last.then_inc(d["turned"], 1)
                            pe.wait_ge(d["copied"], t * (T // 4) + T // 4)
                            for j in range(T):
                                last = nc.tensor.matmul(ps_acc[:, 0:F], d_pt[:, j * P:(j + 1) * P], ranked[:, j, 0:F], start=(j == 0), stop=(j == T - 1))
                            last.then_inc(d["acc"], 1)
                            pe.wait_ge(d["step"], t * STEPS[layer] + STEPS[layer])
                    else:
                        for q in range(T // 4):
                            if q >= 2:
                                pe.wait_ge(d["x_copied"], q - 1)
                            for j in range(4):
                                last = nc.tensor.transpose(ps_tr[q % 2][:, j * P:(j + 1) * P], record[:, 4 * q + j, 0:F], ident[:, :])
                            last.then_inc(d["x_turned"], 1)
                        pe.wait_ge(d["maxed"], 1)
                        for t in range(T):
                            nc.tensor.transpose(ps_mm[0][:, 0:P], d_max_t[:, t * P:(t + 1) * P], ident[:, :]).then_inc(d["back"], 1)
                            pe.wait_ge(d["step"], t * STEPS[layer] + STEPS[layer])

        @block.vector
        def _(dve):
            V = nc.vector
            steps = 0

            def do(ins):
                nonlocal steps
                steps += 1
                ins.then_inc(dve_step, 1)
                return steps

            def after(n=None):
                dve.wait_ge(dve_step, steps if n is None else n)

            do(V.memset(onehot[:, :, :], 0.0))
            do(V.memset(rows_below[:, :, 0:1], 0.0))
            after()
            dve.wait_ge(pool_made, 6)
            def hold(i, ap):
                V.tensor_copy(held_word[:, i:i + 1], ap)

            with dve.Fori(0, QUADS) as quad:
                now = 0

                def did(ins):
                    nonlocal now
                    now += 1
                    ins.then_inc(searched, 1)

                def turned():
                    dve.wait_ge(searched, quad * QUAD_STEPS + now)

                def key(b):
                    dve.wait_ge(folded, quad * QUAD + (b + 1))
                    V.tensor_tensor(key_buf[b], ps_fold[b % 2][:, :], column_w[:, :], ALU.mult).then_inc(keyed, 1)

                def search(b):
                    dve.wait_ge(keyed, quad * QUAD + (b + 1))
                    hold(b, key_buf[b][:, 0:1])
                    part = FOLDED // SEARCHES
                    for e in range(SEARCHES):
                        last = V.max(found[:, 0, b, 8 * e:8 * e + 8], key_buf[b][:, e * part:(e + 1) * part])
                    return last

                def greatest16(out16, held_from, values, left):
                    turned()
                    hold(held_from, values[:, 0, 0:1])
                    for b in range(QUAD):
                        last = V.max(out16[:, b, 0:8], values[:, b, :])
                    did(last)
                    turned()
                    hold(held_from + 1, out16[:, 0, 0:1])
                    for b in range(QUAD):
                        last = V.match_replace(left[:, b, :], out16[:, b, 0:8], values[:, b, :], 0.0)
                    did(last)
                    turned()
                    hold(held_from + 2, left[:, 0, 0:1])
                    for b in range(QUAD):
                        last = V.max(out16[:, b, 8:16], left[:, b, :])
                    did(last)
                    turned()

                key(0)
                key(1)
                search(0)
                key(2)
                search(1)
                key(3)
                search(2)
                did(search(3))
                greatest16(top16, 4, found[:, 0, :, :], found[:, 1, :, :])
                whole, f_bits, product, column = (key_i[:, i, :, :] for i in range(4))
                f_least, f_inverse, quotient = (key_f[:, i, :, :] for i in range(3))
                did(V.tensor_copy(whole, top16[:, :, :])); turned()
                did(V.tensor_single_scalar(f_bits, whole, KEY_SHIFT, op=ALU.logical_shift_right))
                did(V.tensor_single_scalar(product, whole, (1 << KEY_SHIFT) - 1, op=ALU.bitwise_and)); turned()
                did(V.tensor_scalar_max(f_least, f_bits, 1.0)); turned()
                did(V.reciprocal(f_inverse, f_least))
                for k in range(FOLDS):
                    did(V.tensor_scalar(bits[:, k, :, :], f_bits, k, 1, ALU.logical_shift_right, ALU.bitwise_and))
                turned()
                did(V.tensor_tensor(quotient, product, f_inverse, ALU.mult)); turned()
                did(V.tensor_scalar_add(column, quotient, 1.25)); turned()
                for k in range(FOLDS):
                    last = V.scalar_tensor_tensor(edge[:, :, k, :], column, float(k * FOLDED), bits[:, k, :, :], ALU.add, ALU.mult)
                did(last)
                edges = edge[:, :, :, :].rearrange("p b k s -> p b (k s)")
                greatest16(top16, 8, edges, edge_left)
                did(V.tensor_copy(record_i[:, bass.ds(quad * QUAD, QUAD), C_NBR:C_NBR + SLOTS], top16[:, :, :]))
                deg, whole_list, minus = (quad_deg[:, i, :] for i in range(3))
                did(V.tensor_single_scalar(held[:, :, :], top16[:, :, :], 0.0, op=ALU.is_gt)); turned()
                did(V.tensor_reduce(deg, held[:, :, :], AX.X, ALU.add)); turned()
                dve.wait_ge(masked, quad * QUAD + QUAD)
                did(V.tensor_tensor(whole_list, row_sum[:, bass.ds(quad * QUAD, QUAD)], deg, ALU.is_equal)); turned()
                did(V.scalar_tensor_tensor(minus, deg, float(-(SLOTS + 1)), whole_list, ALU.add, ALU.mult))
                did(V.tensor_copy(record[:, bass.ds(quad * QUAD, QUAD), C_DEG], deg)); turned()
                minus_all = minus.unsqueeze(1).to_broadcast([P, LEVELS + 1, QUAD])
                did(V.tensor_tensor(below[:, :, :], minus_all, minus_level[:, :, :], ALU.is_gt))
                did(V.tensor_tensor(onehot[:, :, bass.ds(quad * (PAD + QUAD) + PAD, QUAD)], minus_level[:, 0:LEVELS, :], minus_all[:, 0:LEVELS, :], ALU.is_equal)); turned()
                did(V.tensor_reduce(quad_below[:, :], below[:, :, :], AX.X, ALU.add)); turned()
                did(V.tensor_tensor(rows_below[:, :, bass.ds(quad + 1, 1)], rows_below[:, :, bass.ds(quad, 1)], quad_below[:, :].unsqueeze(2), ALU.add)); turned()
                assert now == QUAD_STEPS, now
            dve.wait_ge(score_copied, 1)
            V.tensor_reduce(best_dst[:, 0:1], record[:, :, C_SDST], AX.X, ALU.max).then_inc(tops_made, 1)
            dve.wait_ge(counted, 1)
            half = LEVELS // 2
            place_q = place[:, :, :].rearrange("p l (q j) -> p l q j", j=QUAD)
            for b, (levels, quads) in enumerate([(slice(0, half), slice(0, QUADS - 1)), (slice(half, LEVELS), slice(0, QUADS - 1)),
                                                 (slice(0, LEVELS), slice(QUADS - 1, QUADS))]):
                to = place_q[:, levels, quads, :]
                l, q = to.shape[1], to.shape[2]
                do(V.tensor_tensor(to, ps_place[b][:, 0:l * q * QUAD].rearrange("p (l q j) -> p l q j", l=l, q=q),
                                   onehot_q[:, levels, quads, PAD:], ALU.mult))
            after()
            do(V.tensor_reduce(rank_f[:, :], place[:, :, :].rearrange("p l t -> p t l"), AX.X, ALU.add)); after()
            V.tensor_copy(rank_i[:, :], rank_f[:, :]).then_inc(ranks_made, 1)
            V.tensor_scalar_add(record[:, :, C_RANK], rank_f[:, :], 1.0).then_inc(ranks_made, 1)
            dve.wait_ge(pool_made, POOL_MADE)
            more = slice(2, 2 + PACKED)
            do(V.tensor_reduce(packed_rows[:, :], ps_below[:, more], AX.X, ALU.add))
            do(V.tensor_tensor(over[:, 0:LEVELS - 1], ps_below[:, 1:LEVELS], caps[:, :], ALU.is_gt))
            do(V.tensor_single_scalar(over[:, LEVELS - 1:LEVELS], ps_below[:, LEVELS - 1:LEVELS], float(N - P), op=ALU.is_lt))
            after(steps - 2)
            do(V.tensor_single_scalar(over[:, LEVELS:LEVELS + 1], packed_rows[:, :], float(P), op=ALU.is_gt))
            after()
            do(V.tensor_reduce(flag_f[:, :], over[:, :], AX.X, ALU.add)); after()
            V.tensor_copy(flag_i[:, :], flag_f[:, :]).then_inc(flag_made, 1)
            dve.wait_ge(flag_made, 1)
            big_degree = dve.value_load(flag_i[0:1, 0:1], min_val=0, max_val=64)
            with dve.If(big_degree == 0):
                LAST = T - 1

                def bc(ap, shape, axis):
                    return ap.unsqueeze(axis).to_broadcast(shape)

                do(V.memset(pack_start[:, 0:1], 0.0)); after()
                for k in range(PACKED):
                    rows = ps_below[:, PACKED + 1 - k:PACKED + 2 - k]
                    do(V.tensor_tensor(pack_start[:, k + 1:k + 2], pack_start[:, k:k + 1], rows, ALU.add)); after()
                lane = lane_minus_row_t[:, 0:1]
                do(V.tensor_scalar(in_part[:, 0, :], pack_start[:, 0:PACKED], lane, None, ALU.is_le))
                do(V.tensor_scalar(in_part[:, 1, :], pack_start[:, 1:PACKED + 1], lane, None, ALU.is_gt)); after()
                do(V.tensor_tensor(in_part[:, 2, :], in_part[:, 0, :], in_part[:, 1, :], ALU.mult)); after()
                for k in range(PACKED):
                    do(V.tensor_scalar(to_lane[:, k, :], lane_minus_row[:, :], pack_start[:, k:k + 1], None, ALU.is_equal))
                    do(V.tensor_scalar(to_row[:, k, :], lane_minus_row_t[:, :], pack_start[:, k:k + 1], in_part[:, 2, k:k + 1],
                                       ALU.is_equal, ALU.mult))
                dve.wait_ge(lists_loaded, 16)
                do(V.tensor_copy(packed_nbr[:, :], ranked_i[:, 0, C_NBR + len(SERVED):C_NBR + SLOTS])); after()
                V.tensor_single_scalar(missing[:, 0, :], packed_nbr[:, :], 0.0, op=ALU.is_equal).then_inc(pack_made, 1)
                dve.wait_ge(pack_made, 1)
                do(V.tensor_single_scalar(missing[:, 1, :], missing[:, 0, :], FAR, op=ALU.mult))
                do(V.tensor_single_scalar(missing[:, 2, :], missing[:, 0, :], LOWEST, op=ALU.mult))
                dve.wait_ge(packed, 1)
                V.tensor_copy(packed_index[:, :], ps_packed).then_inc(packed_ready, 1)

                dve.wait_ge(lists_loaded, 16)
                dve.wait_ge(best_made, 1)
                V.tensor_scalar(diag[:, :], ident[:, :], ranked[:, LAST, C_SSRC:C_SSRC + 1], None, ALU.mult).then_inc(diag_made, 1)
                do(V.tensor_single_scalar(has_nbr[:, :], ranked[:, :, C_DEG], 0.0, op=ALU.is_gt)); after()
                do(V.tensor_scalar(no_nbr[:, :], has_nbr[:, :], -1.0, 1.0, ALU.mult, ALU.add))
                dve.wait_ge(src_spread, 1)
                src_row = ps_small[:, 128:256]
                do(V.tensor_scalar_add(row_max[:, 0, :], src_row, best_dst[:, 1:2])); after()
                do(V.scalar_tensor_tensor(row_max[:, 1, :], row_max[:, 0, :], SLOPE, row_max[:, 0, :], ALU.mult, ALU.max)); after()
                do(V.tensor_scalar_add(row_max[:, 0, :], row_max[:, 1, :], MASKED)); after()
                flat = big[:, 0, 0:T * F]
                do(V.tensor_tensor(weights_t, bc(src_row, [P, T, P], 1), bc(record[:, :, C_SDST], [P, T, P], 2), ALU.add)); after()
                do(V.scalar_tensor_tensor(flat, flat, SLOPE, flat, ALU.mult, ALU.max)); after()
                do(V.tensor_scalar_add(flat, flat, MASKED)); after()
                V.tensor_tensor(weights_t, weights_t, bc(row_max[:, 0, :], [P, T, P], 1), ALU.subtract).then_inc(lone_scored, 1)

                norms = 0

                def y_free(layer, g):
                    if g >= 2:
                        dve.wait_ge(layer_done[layer], g - 1)
                    elif layer:
                        dve.wait_ge(layer_done[layer - 1], len(GROUPS))

                def norm(layer, g):
                    n = GROUPS[g][1]
                    nonlocal norms
                    for i in range(n):
                        do(V.bn_stats(moments[:, i, :], y[:, g % 2, i, :]))
                    after()
                    for i in range(n):
                        do(V.bn_aggr(mean_var[:, i, :], moments[:, i, :]))
                    after()
                    V.tensor_scalar_add(stat[:, 5, 0:n], mean_var[:, 0:n, 1], EPS).then_inc(variance_ready, 1)
                    norms += 1
                    dve.wait_ge(deviation_ready, norms)
                    do(V.reciprocal(norm_scale[:, g % 2, 0:n], stat[:, 6, 0:n])); after()
                    V.scalar_tensor_tensor(norm_shift[:, g % 2, 0:n], mean_var[:, 0:n, 0], -1.0, norm_scale[:, g % 2, 0:n],
                                           ALU.mult, ALU.mult).then_inc(shift_ready, 1)

                def attention(layer, width, s_src, first):
                    def scores(g):
                        t0, n, depth, s0 = GROUPS[g]
                        dve.wait_ge(gathered[g], 16 * slots(g) * (layer + 1))
                        got = gat(width, s0, slots(g)).rearrange("p (s f) -> p s f", f=width)
                        rows = got[:, 0:n * depth, :].rearrange("p (t k) f -> p t k f", t=n)
                        z = score[:, g % 2, 0:n * list_slots(g)]
                        z3 = z.rearrange("p (t k) -> p t k", t=n)
                        do(V.tensor_tensor(z3[:, :, 0:depth], rows[:, :, :, C_SDST], bc(s_src[:, t0:t0 + n], [P, n, depth], 2), ALU.add))
                        if layer == 0:
                            do(V.tensor_copy(nbr_rank[:, s0:s0 + slots(g)], got[:, :, C_RANK]))
                        if g == FIRST:
                            dve.wait_ge(unpacked, layer + 1)
                            for k in range(0, PACKED, 3):
                                m = min(3, PACKED - k)
                                dst = ps_unpack[k // 3][:, 0:m * width].rearrange("p (k f) -> p k f", k=m)[:, :, C_SDST]
                                do(V.scalar_tensor_tensor(z[:, depth + k:depth + k + m], dst, s_src[:, t0:t0 + 1],
                                                          missing[:, 1, k:k + m], ALU.add, ALU.add))
                        after()
                        do(V.scalar_tensor_tensor(z, z, SLOPE, z, ALU.mult, ALU.max)); after()
                        do(V.tensor_reduce(stat[:, g % 2, 0:n], z3, AX.X, ALU.max)); after()
                        V.tensor_tensor(z3, z3, bc(stat[:, g % 2, 0:n], [P, n, list_slots(g)], 2), ALU.subtract).then_inc(scores_ready, 1)

                    def weigh(g):
                        t0, n, depth, s0 = GROUPS[g]
                        dve.wait_ge(exps_ready, first + g + 1)
                        rows = gat(width, s0, n * depth).rearrange("p (s f) -> p s f", f=width)[:, :, 0:F]
                        depth = list_slots(g)
                        p2 = score[:, g % 2, 0:n * depth]
                        do(V.tensor_reduce(stat[:, 2, 0:n], p2.rearrange("p (t k) -> p t k", t=n), AX.X, ALU.add))
                        sums = steps
                        y_free(layer, g)
                        def row(s):
                            if g == FIRST and s >= len(SERVED):
                                return unpacked_row(s - len(SERVED), width)[:, 0:F]
                            return rows[:, s, :]

                        sums_of = [y[:, g % 2, i, :] for i in range(n)]
                        if n == 1:
                            sums_of.append(odd_slots[:, :])
                        for s in range(n * depth):
                            i, k = (0, s) if n == 1 else (s % n, s // n)
                            acc, at = sums_of[s % len(sums_of)], i * depth + k
                            if s < len(sums_of):
                                do(V.tensor_scalar(acc, row(at), p2[:, at:at + 1], None, ALU.mult))
                            else:
                                after(steps - len(sums_of) + 1)
                                do(V.scalar_tensor_tensor(acc, row(at), p2[:, at:at + 1], acc, ALU.mult, ALU.add))
                            if s == len(sums_of) - 1:
                                after(sums)
                                do(V.reciprocal(stat[:, 3, 0:n], stat[:, 2, 0:n]))
                        if n == 1:
                            after()
                            do(V.tensor_tensor(sums_of[0], sums_of[0], sums_of[1], ALU.add))
                        after()
                        for i in range(n):
                            do(V.scalar_tensor_tensor(y[:, g % 2, i, :], y[:, g % 2, i, :], stat[:, 3, i:i + 1], ranked[:, t0 + i, 0:F], ALU.mult, ALU.add))
                        after()
                        if t0 + n == T:
                            i = n - 1
                            do(V.scalar_tensor_tensor(y[:, g % 2, i, :], (lone if layer == 0 else h_mean)[:, :], no_nbr[:, LAST:T],
                                                      y[:, g % 2, i, :], ALU.mult, ALU.add)); after()
                        norm(layer, g)

                    for g in range(len(GROUPS)):
                        scores(g)
                        if GROUPS[g][0] + GROUPS[g][1] == T and layer == 0:
                            dve.wait_ge(lone_summed, 1)
                            do(V.reciprocal(lone_sum[:, :], ps_small[:, 256:257])); after()
                            do(V.tensor_scalar(lone[:, :], ps_acc[:, 0:F], lone_sum[:, :], None, ALU.mult)); after()
                        weigh(g)

                def neighbour_max(layer):
                    for g, (t0, n, depth, s0) in enumerate(GROUPS):
                        dve.wait_ge(gathered[g], 16 * slots(g) * (layer + 1))
                        rows = gat(F, s0, n * depth).rearrange("p (t k f) -> p t f k", t=n, k=depth)
                        own = ranked[:, t0:t0 + n, 0:F]
                        y_free(layer, g)
                        if depth > 1:
                            do(V.tensor_reduce(y[:, g % 2, 0:n, :], rows, AX.X, ALU.max)); after()
                            if g == FIRST:
                                dve.wait_ge(unpacked, layer + 1)
                                for k in range(PACKED):
                                    do(V.scalar_tensor_tensor(y[:, g % 2, 0, :], unpacked_row(k, F), missing[:, 2, k:k + 1], y[:, g % 2, 0, :],
                                                              ALU.add, ALU.max)); after()
                            do(V.tensor_tensor(y[:, g % 2, 0:n, :], y[:, g % 2, 0:n, :], own, ALU.add)); after()
                        else:
                            for i in range(n):
                                do(V.scalar_tensor_tensor(y[:, g % 2, i, :], rows[:, i, :, 0], has_nbr[:, t0 + i:t0 + i + 1],
                                                          ranked[:, t0 + i, 0:F], ALU.mult, ALU.add))
                            after()
                        norm(layer, g)

                dve.wait_ge(x_ranked, 16)
                attention(0, W0, ranked[:, :, C_SSRC], 0)
                neighbour_max(1)
                neighbour_max(2)
                dve.wait_ge(mean_made, 1)
                do(V.tensor_copy(h_mean[:, :], ps_acc[:, 128:128 + F])); after()
                attention(3, W3, h[:, :, F + 1], len(GROUPS))
            with dve.Else():
                for layer in range(4):
                    d = DENSE[layer]

                    turn_steps = 0

                    def did(ins):
                        nonlocal turn_steps
                        turn_steps += 1
                        ins.then_inc(d["step"], 1)

                    def turned(t):
                        dve.wait_ge(d["step"], t * STEPS[layer] + turn_steps)

                    def finish(t, agg, scale):
                        did(V.tensor_copy(d_own[:, :], record[:, bass.ds(t, 1), 0:F].rearrange("p a f -> p (a f)"))); turned(t)
                        if scale is None:
                            did(V.tensor_tensor(d_y[:, 0, :], agg, d_own[:, :], ALU.add)); turned(t)
                        else:
                            did(V.scalar_tensor_tensor(d_y[:, 0, :], agg, scale, d_own[:, :], ALU.mult, ALU.add)); turned(t)
                        did(V.bn_stats(d_mom[:, :], d_y[:, 0, :])); turned(t)
                        did(V.tensor_copy(d_col[:, 6:7], d_mom[:, 0:1]))
                        did(V.bn_aggr(d_mv[:, :], d_mom[:, :])); turned(t)
                        V.tensor_scalar_add(d_col[:, 3:4], d_mv[:, 1:2], EPS).then_inc(d["var"], 1)
                        dve.wait_ge(d["dev"], t + 1)
                        did(V.reciprocal(d_col[:, 5:6], d_col[:, 4:5])); turned(t)
                        did(V.tensor_scalar(d_y[:, 1, :], d_y[:, 0, :], d_mv[:, 0:1], d_col[:, 5:6], ALU.subtract, ALU.mult)); turned(t)
                        assert turn_steps == STEPS[layer], (layer, turn_steps)

                    if layer:
                        dve.wait_ge(d["x_in"], 16)
                    if layer in (0, 3):
                        if layer == 0:
                            dve.wait_ge(ranks_made, 2)
                            dve.wait_ge(score_copied, 1)
                            V.tensor_copy(ranked[:, :, 0:W0], record[:, :, 0:W0]).then_inc(d["v_ready"], 1)
                        dve.wait_ge(d["v_ready"], 1 if layer == 0 else T)
                        dve.wait_ge(d["dst_in"], 16)
                        with dve.Fori(0, T) as t:
                            turn_steps = 0
                            did(V.tensor_copy(d_col[:, 0:1], ranked[:, bass.ds(t, 1), C_SSRC])); turned(t)
                            did(V.tensor_scalar(d_e, d_dst, d_col[:, 0:1], None, ALU.add)); turned(t)
                            did(V.scalar_tensor_tensor(d_e, d_e, SLOPE, d_e, ALU.mult, ALU.max))
                            dve.wait_ge(d["adj"], t * 16 + 16)
                            did(V.tensor_single_scalar(d_m, d_adj[0], 0.0, op=ALU.is_gt)); turned(t)
                            low = -MASKED if layer == 0 else 9e15
                            if layer == 3:
                                did(V.tensor_tensor(d_e, d_e, d_m, ALU.mult)); turned(t)
                            did(V.tensor_scalar(d_m, d_m, low, -low, ALU.mult, ALU.add)); turned(t)
                            did(V.tensor_tensor(d_e, d_e, d_m, ALU.add)); turned(t)
                            did(V.tensor_reduce(d_col[:, 1:2], d_e, AX.X, ALU.max, negate=True)); turned(t)
                            V.tensor_copy(d_col[:, 7:8], d_col[:, 1:2]).then_inc(d["score"], 1)
                            dve.wait_ge(d["exp"], t + 1)
                            did(V.reciprocal(d_col[:, 7:8], d_col[:, 2:3])); turned(t)
                            dve.wait_ge(d["acc"], t + 1)
                            finish(t, ps_acc[:, 0:F], d_col[:, 7:8])
                            dve.wait_ge(d["stored"], t * 16 + 16)
                    else:
                        dve.wait_ge(d["x_copied"], T // 4)
                        rows = (d["row_even"], d["row_odd"])
                        with dve.Fori(0, N // 2) as pair:
                            for b in range(2):
                                dve.wait_ge(rows[b], pair * 16 + 16)
                                V.tensor_scalar(d_e, d_adj[b], 0.0, LOWEST, ALU.is_equal, ALU.mult).then_inc(d["row_read"], 1)
                                dve.wait_ge(d["row_read"], pair * 2 + (b + 1))
                                V.tensor_reduce(d_has[:, bass.ds(pair * 2 + b, 1)], d_e, AX.X, ALU.max).then_inc(d["row_step"], 1)
                                V.tensor_tensor(d_m, d_e, d_xt, ALU.add).then_inc(d["row_step"], 1)
                                dve.wait_ge(d["row_step"], pair * 6 + (3 * b + 2))
                                V.tensor_reduce(d_max_t[:, bass.ds(pair * 2 + b, 1)], d_m, AX.X, ALU.max).then_inc(d["row_step"], 1)
                                dve.wait_ge(d["row_step"], pair * 6 + (3 * b + 3))
                        V.tensor_single_scalar(d_m, d_has, 0.0, op=ALU.is_equal).then_inc(d["row_read"], 1)
                        dve.wait_ge(d["row_read"], N + 1)
                        V.tensor_tensor(d_max_t, d_max_t, d_m, ALU.mult).then_inc(d["maxed"], 1)
                        with dve.Fori(0, T) as t:
                            turn_steps = 0
                            dve.wait_ge(d["back"], t + 1)
                            finish(t, ps_mm[0][:, 0:P], None)
                            dve.wait_ge(d["stored"], t * 16 + 16)


_INS = ["x", "adj", "L0_gnn_attn", "L3_gnn_W", "L3_gnn_a"]


def kernel(**inputs):
    import numpy as _np
    import concourse.bacc as _bacc
    from concourse import mybir as _mybir
    from concourse.bass_utils import run_bass_kernel_spmd as _run

    nc = _bacc.Bacc("TRN2", target_bir_lowering=False, num_devices=1)
    arrays, args = {}, []
    for name in _INS:
        a = _np.ascontiguousarray(inputs[name])
        arrays[f"in_{name}_dram"] = a
        args.append(nc.dram_tensor(f"in_{name}_dram", a.shape, _mybir.dt.from_np(a.dtype), kind="ExternalInput").ap())
    args.append(nc.dram_tensor("out_0_dram", (4096, 128), _mybir.dt.float32, kind="ExternalOutput").ap())
    gnn_kernel(nc, *args)
    r = _run(nc, [arrays], core_ids=[0])
    return r.results[0]["out_0_dram"]
```
